# Optimizing a Trainium2 kernel written in Bass

```python
import numpy as np
import jax
import jax.numpy as jnp

def _softmax(x, axis=-1):
    return jax.nn.softmax(x, axis=axis)

def _gelu(x):
    return jax.nn.gelu(x, approximate=True)

def _silu(x):
    return jax.nn.silu(x)

def _sigmoid(x):
    return jax.nn.sigmoid(x)

def _layernorm(x, axis=-1, eps=1e-05):
    m = jnp.mean(x, axis=axis, keepdims=True)
    v = jnp.var(x, axis=axis, keepdims=True)
    return (x - m) / jnp.sqrt(v + eps)

def _scatter_add(tgt, idx, src, axis=0):
    return tgt.at[idx].add(src)

def _segment_sum(src, seg, n):
    return jax.ops.segment_sum(src, seg, n)
kernel_name = 'mk_seq_postln_d1_jaxref_r4_a7640d'

def setup_inputs(seed: int=0):
    np.random.seed(seed)
    _w = jnp.asarray

    def _L0_attn_setup():
        import jax, jax.numpy as jnp
        import numpy as np
        B, S, D, H = (2, 512, 512, 16)
        HD = D // H
        key = jax.random.key(seed)
        kx, kq, kk, kv, ko = jax.random.split(key, 5)
        scale = 1.0 / np.sqrt(D)
        return {'x': jax.random.normal(kx, (B, S, D), dtype=jnp.float32), 'wq': jax.random.normal(kq, (D, D), dtype=jnp.float32) * scale, 'wk': jax.random.normal(kk, (D, D), dtype=jnp.float32) * scale, 'wv': jax.random.normal(kv, (D, D), dtype=jnp.float32) * scale, 'wo': jax.random.normal(ko, (D, D), dtype=jnp.float32) * scale}
    _L0_attn_in = _L0_attn_setup()

    def _L0_ffn_setup():
        import jax, jax.numpy as jnp
        import numpy as np
        RANK = 64
        SCALING = 1.0 / RANK
        TEMPERATURE = 1.0
        key = jax.random.key(seed)
        k_x, k_a, k_b, k_w = jax.random.split(key, 4)
        B_, S, D = (4, 512, 512)
        E, R, O = (8, RANK, 512)
        x = jax.random.normal(k_x, (B_, S, D), dtype=jnp.float32)
        A = jax.random.normal(k_a, (E, R, D), dtype=jnp.float32) * (1.0 / np.sqrt(D))
        Bw = jax.random.normal(k_b, (E, O, R), dtype=jnp.float32) * 0.02
        Wr = jax.random.normal(k_w, (E, D), dtype=jnp.float32) * (1.0 / np.sqrt(D))
        br = jnp.zeros((E,), dtype=jnp.float32)
        return {'x': x, 'A': A, 'B': Bw, 'Wr': Wr, 'br': br}
    _L0_ffn_in = _L0_ffn_setup()
    _d = {'L0_attn_x': _L0_attn_in['x'], 'L0_attn_wq': _L0_attn_in['wq'], 'L0_attn_wk': _L0_attn_in['wk'], 'L0_attn_wv': _L0_attn_in['wv'], 'L0_attn_wo': _L0_attn_in['wo'], 'L0_ffn_A': _L0_ffn_in['A'], 'L0_ffn_B': _L0_ffn_in['B'], 'L0_ffn_Wr': _L0_ffn_in['Wr'], 'L0_ffn_br': _L0_ffn_in['br']}
    _x0 = _d['L0_attn_x']
    _d['L0_attn_x'] = jax.random.normal(jax.random.fold_in(jax.random.key(seed), 1), (4, 1024, 512), dtype=_x0.dtype)
    del _x0
    return _d

def reference(L0_attn_x, L0_attn_wq, L0_attn_wk, L0_attn_wv, L0_attn_wo, L0_ffn_A, L0_ffn_B, L0_ffn_Wr, L0_ffn_br):

    def _L0_attn_ref(x, wq, wk, wv, wo):
        import jax, jax.numpy as jnp
        import numpy as np
        B, S, D, H = (2, 512, 512, 16)
        HD = D // H
        bsz, seqlen, dim = x.shape
        xq = (x @ wq.T).reshape(bsz, seqlen, H, HD)
        xk = (x @ wk.T).reshape(bsz, seqlen, H, HD)
        xv = (x @ wv.T).reshape(bsz, seqlen, H, HD)
        scores = jnp.einsum('bqhd,bkhd->bhqk', xq, xk)
        probs = jax.nn.softmax(scores.astype(jnp.float32), axis=-1).astype(xq.dtype)
        out = jnp.einsum('bhqk,bkhd->bqhd', probs, xv).reshape(bsz, seqlen, dim)
        return out @ wo.T

    def _L0_ffn_ref(x, A, B, Wr, br):
        import jax, jax.numpy as jnp
        import numpy as np
        RANK = 64
        SCALING = 1.0 / RANK
        TEMPERATURE = 1.0
        batch, seq, d = x.shape
        E, out_dim = (B.shape[0], B.shape[1])
        x_flat = x.reshape(-1, d)
        logits = (x_flat @ Wr.T + br) / TEMPERATURE
        probs = jax.nn.softmax(logits, axis=-1)
        expert_idx = jnp.argmax(probs, axis=-1)
        expert_weight = jnp.max(probs, axis=-1)
        h = jnp.einsum('nd,erd->ner', x_flat, A)
        y = jnp.einsum('ner,eor->neo', h, B) * SCALING
        sel = jnp.take_along_axis(y, expert_idx[:, None, None], axis=1)[:, 0, :]
        out_flat = sel * expert_weight[:, None]
        return out_flat.reshape(batch, seq, out_dim)
    x = L0_attn_x
    x = _layernorm(x + _L0_attn_ref(x, L0_attn_wq, L0_attn_wk, L0_attn_wv, L0_attn_wo), axis=-1)
    x = _layernorm(x + _L0_ffn_ref(x, L0_ffn_A, L0_ffn_B, L0_ffn_Wr, L0_ffn_br), axis=-1)
    return x

_drawn_inputs = setup_inputs


def setup_inputs(seed=0):
    import zlib

    import numpy as np

    out = dict(_drawn_inputs(seed))
    spreads = {'L0_ffn_br': (0.0, 0.8)}
    factors = {'L0_ffn_A': 8.0, 'L0_ffn_B': 8.0, 'L0_ffn_Wr': 8.0}
    for name, (base, spread) in spreads.items():
        noise = np.random.default_rng([zlib.crc32(name.encode()), seed]).standard_normal(out[name].shape)
        drawn = base * np.exp(spread * noise) if base else spread * noise
        out[name] = jnp.asarray(drawn.astype(out[name].dtype))
    for name, factor in factors.items():
        out[name] = (out[name] * factor).astype(out[name].dtype)
    return out
```

```python
from contextlib import ExitStack

import concourse.bass as bass
from concourse import mybir


def build_attention_lora_moe_block(nc, xT, x, wqT, wkT, wvT, woT, aT, bT, wrT, br, out):
    f32, f32r = mybir.dt.float32, mybir.dt.float32r
    ALU, ACT, AX = mybir.AluOpType, mybir.ActivationFunctionType, mybir.AxisListType

    D, TOK = xT.shape
    B, S, _ = x.shape
    E = br.shape[1]
    R = aT.shape[1] // E
    HD = 32
    H = D // HD
    KT = D // 128
    QC = S // 512
    KB = S // 128
    PAIRS = H // 2
    QUADS = H // 4
    UNITS = 2 * KB
    MAXES = 2 * KB * QC
    KS = 3 * HD + 2
    NSTACK, NP, NSC = 3, 6, 3
    START = 1
    EPS, SCALING = 1e-5, 1.0 / R
    PART_DMAS = 6
    NPROJ = 4 * QUADS + KB

    ctx = ExitStack()
    with ctx:
        def sb(name, shape, dt=f32):
            return ctx.enter_context(nc.sbuf_tensor(name, shape, dt))

        def ps(name, shape):
            return ctx.enter_context(nc.psum_tensor(name, shape, f32))

        def sem(name):
            return ctx.enter_context(nc.semaphore(name))

        wq_s, wk_s, wv_s, wo_s = (sb(n, [128, KT, D]) for n in ("wq_s", "wk_s", "wv_s", "wo_s"))
        a_s, b_s = sb("a_s", [128, KT, E * R]), sb("b_s", [128, KT, D])
        wr_s, br_s = sb("wr_s", [128, KT, E]), sb("br_s", [1, E])
        xT_s = sb("xT_s", [128, KT, S])
        nat = {n: sb(n, [128, S], f32r) for n in ("q_hi", "q_lo", "k_hi", "k_lo")}
        kS, qS = sb("kS", [128, NSTACK, 2, S], f32r), sb("qS", [128, NSTACK, 2, S], f32r)
        V = sb("V", [128, KB, D])
        P = sb("P", [128, NP, S])
        Psum = sb("Psum", [128, 2, 2, S])
        attT = sb("attT", [128, KT, S])
        pv_s, rden = sb("pv_s", [128, 512]), sb("rden", [128, 512])
        xt = [P[:, 0, 512 * i:512 * i + 512] for i in range(2)]
        z_s = [P[:, 1, 512 * i:512 * i + 512] for i in range(2)]
        y = [P[:, 2 + i // 2, 512 * (i % 2):512 * (i % 2) + 512] for i in range(3)]
        yT = P[:, 3, 512:1024]
        hm = P[:, 4, 0:512]
        hmT = P[:, 4, 512:1024]
        mxc = sb("mxc", [128, 2, MAXES])
        mm = sb("mm", [128, 2 * KB])
        nm = sb("nm", [128, 2, 2 * KB], f32r)
        mrow = sb("mrow", [32, 128], f32r)
        ident = sb("ident", [128, 128])
        ones = sb("ones", [128, 32])
        ones_row = sb("ones_row", [1, 128])
        rank = sb("rank", [128, E])
        mhalf = sb("mhalf", [128, 1])
        settle, eps_s = sb("settle", [128, 1]), sb("eps_s", [128, 1])
        st1, st2 = sb("st1", [128, 6]), sb("st2", [128, 6])
        mv1, mv2 = sb("mv1", [128, 2]), sb("mv2", [128, 2])
        ve1, ve2 = sb("ve1", [128, 1]), sb("ve2", [128, 1])
        rs1, rs2 = sb("rs1", [128, 1]), sb("rs2", [128, 1])
        lmax, nlmax = sb("lmax", [128, 1]), sb("nlmax", [128, 1])
        lexp, lsum, lrec = sb("lexp", [128, E]), sb("lsum", [128, 1]), sb("lrec", [128, 1])
        eq, eqm, gate = sb("eq", [128, E]), sb("eqm", [128, 1]), sb("gate", [128, E])

        sc = [ps(f"sc{i}", [128, 512]) for i in range(NSC)]
        pv, den, w = ps("pv", [128, 512]), ps("den", [128, 512]), ps("w", [128, 512])
        mx = [ps(f"mx{i}", [128, 512]) for i in range(2)]
        o_ps, t1_ps, h_ps, l_ps, t2_ps, z_ps = sc[0], sc[1], sc[2], pv, w, mx[0]

        const_ready, x_loaded = sem("const_ready"), sem("x_loaded")
        w_loaded = {n: sem(f"{n}_loaded") for n in ("wq", "wk", "wv", "tail_w")}
        proj_ready, hi_done, lo_done, v_done = sem("proj_ready"), sem("hi_done"), sem("lo_done"), sem("v_done")
        stack_loaded, m_loaded = [sem(f"stack_loaded{i}") for i in range(NSTACK)], sem("m_loaded")
        mx_ready, mx_done, comb_done = sem("mx_ready"), sem("mx_done"), sem("comb_done")
        mt_ready, mrow_done = sem("mt_ready"), sem("mrow_done")
        sc_ready, exp_done, pv_done, pv_copied = sem("sc_ready"), sem("exp_done"), sem("pv_done"), sem("pv_copied")
        psum_done, den_done, rden_done, norm_done = sem("psum_done"), sem("den_done"), sem("rden_done"), sem("norm_done")
        xt_loaded, o_ready, o_read, stat1, rstd1 = [sem(f"xt_loaded{i}") for i in range(2)], sem("o_ready"), sem("o_read"), sem("stat1"), sem("rstd1")
        y_done, t1_ready, yT_done, h_ready = sem("y_done"), sem("t1_ready"), sem("yT_done"), sem("h_ready")
        nlmax_done, lexp_done, hm_done = sem("nlmax_done"), sem("lexp_done"), sem("hm_done")
        t2_ready, hmT_done, z_ready, z_read = sem("t2_ready"), sem("hmT_done"), sem("z_ready"), sem("z_read")
        stat2, rstd2, out_done, out_stored = sem("stat2"), sem("rstd2"), sem("out_done"), [sem(f"out_stored{i}") for i in range(2)]
        tail_stored = sem("tail_stored")
        tail_step, pool_step = sem("tail_step"), sem("pool_step")

        xT_v = xT.rearrange("(k p) t -> p k t", p=128)

        def x_tile(b, t):
            return x.rearrange("b s d -> (b s) d")[bass.ds(b * S + 128 * t, 128), :]

        def out_tile(b, t):
            return out.rearrange("b s d -> (b s) d")[bass.ds(b * S + 128 * t, 128), :]

        def stacks_there(b, q):
            a_batch = len(range(q % NSTACK, PAIRS, NSTACK))
            return stack_loaded[q % NSTACK], (b * a_batch + q // NSTACK + 1) * 16 * 2 * PART_DMAS

        def unit_kb_head(k):
            return k // 2, k % 2

        def pool_sums_until(unit):
            p, k = divmod(unit, UNITS)
            return 8 * p + 2 * (k // 4) + k % 2 + 1

        AHEAD = 4
        QK_SLOTS = {1: 2, 3: 3}

        def proj_pieces(k):
            if k >= 12:
                return None
            return k // 3, ([0, 1], [2], [3])[k % 3]

        def max_items(p, k):
            q, m = (p + 1, 2 * (k + AHEAD)) if k < UNITS - AHEAD else (p + 2, 2 * (k + AHEAD - UNITS))
            return [(q, m), (q, m + 1)] if q < PAIRS else []

        def start(engine, *semaphores):
            for s in semaphores:
                engine.sem_inc(s, START)

        block = ctx.enter_context(nc.Block())

        @block.sync
        def _(sp):
            start(sp, tail_stored)
            sp.dma_start(xT_s[:, :, :], xT_v[:, :, 0:S]).then_inc(x_loaded, 16)

            def load_stacks(b, q):
                sp.wait_ge(lo_done, b * 4 * QUADS + 4 * (q // 2) + 4 + START)
                if q < NSTACK:
                    sp.wait_ge(sc_ready, b * PAIRS * 2 * UNITS + START)
                at = 64 * (q % 2)
                for stack, parts in ((kS, ("k_hi", "k_lo", "k_hi")), (qS, ("q_hi", "q_hi", "q_lo"))):
                    for n, part in enumerate(parts):
                        for i in range(2):
                            sp.dma_start(stack[HD * n:HD * n + HD, q % NSTACK, i, :].bitcast(f32),
                                         nat[part][at + HD * i:at + HD * i + HD, :].bitcast(f32)).then_inc(stack_loaded[q % NSTACK], 16)

            def load_max(b, q):
                sp.wait_ge(mrow_done, b * PAIRS + q + 1 + START)
                for n in range(2):
                    sp.dma_start(qS[3 * HD + n:3 * HD + n + 1, q % NSTACK, :, :].bitcast(f32)
                                 .rearrange("a i (r t) -> a (i r) t", t=128),
                                 mrow[16 * n:16 * n + 16, :].bitcast(f32)).then_inc(m_loaded, 16)

            with sp.Fori(0, B) as b:
                following = sp.snap((b + 1) % B * S)
                load_stacks(b, 0)
                load_stacks(b, 1)
                load_max(b, 0)
                for p in range(PAIRS):
                    if p + 2 < PAIRS:
                        load_stacks(b, p + 2)
                    if p + 1 < PAIRS:
                        load_max(b, p + 1)
                    if p == 4:
                        sp.wait_ge(proj_ready, b * NPROJ + NPROJ + START)
                        sp.dma_start(xT_s[:, :, :], xT_v[:, :, bass.ds(following, S)]).then_inc(x_loaded, 16)
                sp.wait_ge(pv_done, b * PAIRS * KB + PAIRS * KB + START)
                sp.wait_ge(psum_done, b * 8 * PAIRS + 8 * PAIRS + START)
                for t in range(-2, KB + 2):
                    if t + 2 < KB:
                        if t >= 0:
                            sp.wait_ge(y_done, b * KB + t + 1 + START)
                        sp.dma_start(xt[t % 2], x_tile(b, t + 2)).then_inc(xt_loaded[t % 2], 16)
                    if t >= 2:
                        sp.wait_ge(out_done, b * KB + t - 1 + START)
                        sp.dma_start(out_tile(b, t - 2), z_s[t % 2]).then_inc(out_stored[t % 2], 16)
                for stored in out_stored:
                    sp.wait_ge(stored, (b + 1) * (16 * KB // 2))
                sp.sem_inc(tail_stored, 1)
            sp.wait_ge(x_loaded, 16 * (B + 1))

        @block.gpsimd
        def _(pool):
            start(pool, psum_done, rstd1, rstd2, pool_step)
            pool.dma_start(wk_s[:, :, :], wkT.rearrange("(k p) n -> p k n", p=128)).then_inc(w_loaded["wk"], 16)
            pool.dma_start(wv_s[:, :, :], wvT.rearrange("(k p) n -> p k n", p=128)).then_inc(w_loaded["wv"], 16)
            for s, d in ((wo_s, woT), (a_s, aT), (b_s, bT), (wr_s, wrT)):
                pool.dma_start(s[:, :, :], d.rearrange("(k p) n -> p k n", p=128)).then_inc(w_loaded["tail_w"], 16)
            pool.dma_start(br_s[:, :], br).then_inc(w_loaded["tail_w"], 16)
            pool.memset(ident[:, :], 0.0).then_inc(pool_step, 1)
            pool.memset(ones[:, :], 1.0).then_inc(const_ready, 1)
            pool.memset(ones_row[:, :], 1.0).then_inc(const_ready, 1)
            pool.memset(mhalf[:, :], -0.5).then_inc(const_ready, 1)
            pool.memset(eps_s[:, :], EPS).then_inc(const_ready, 1)
            for e in range(E):
                pool.memset(rank[:, e:e + 1], float(E - e)).then_inc(const_ready, 1)
            pool.wait_ge(pool_step, 1 + START)
            pool.affine_select(out=ident[:, :], in_=ident[:, :], compare_op=ALU.not_equal, fill=1.0,
                               base=0, pattern=[[-1, 128]], channel_multiplier=1).then_inc(const_ready, 1)
            pool.wait_ge(const_ready, 6 + E)

            with pool.Fori(0, B) as b:
                for p in range(PAIRS):
                    for j in range(KB // 2):
                        for i in range(2):
                            u = UNITS * p + 4 * j + i
                            g = 4 * p + j
                            pool.wait_ge(exp_done, b * PAIRS * 2 * UNITS + 2 * (u + 2) + 2 + START)
                            pool.wait_ge(den_done, b * 4 * PAIRS + max(0, g - 1) + START)
                            pool.tensor_tensor(Psum[:, g % 2, i, :], P[:, u % NP, :], P[:, (u + 2) % NP, :],
                                               ALU.add).then_inc(psum_done, 1)
                for t in range(KB + 2):
                    if t < KB:
                        pool.wait_ge(stat1, b * KB + t + 1 + START)
                        pool.tensor_tensor(ve1[:, :], mv1[:, 1:2], eps_s[:, :], ALU.add).then_inc(pool_step, 1)
                        pool.wait_ge(pool_step, b * 2 * KB + 1 + (t + 1) + max(0, t - 2) + START)
                        pool.tensor_tensor(rs1[:, :], ve1[:, :], mhalf[:, :], ALU.pow).then_inc(rstd1, 1)
                    if t >= 2:
                        pool.wait_ge(stat2, b * KB + t - 1 + START)
                        pool.tensor_tensor(ve2[:, :], mv2[:, 1:2], eps_s[:, :], ALU.add).then_inc(pool_step, 1)
                        pool.wait_ge(pool_step, b * 2 * KB + 1 + min(t + 1, KB) + t - 1 + START)
                        pool.tensor_tensor(rs2[:, :], ve2[:, :], mhalf[:, :], ALU.pow).then_inc(rstd2, 1)

        @block.tensor
        def _(pe):
            def qk_group(b, g, n, chunks):
                at = (4 * g + n) if g < 2 else (4 * g + n + KB)
                ws, c = (wq_s, wk_s)[n // 2], n % 2
                bank = (w, pv)[at % 2] if g < 2 else w
                for kt in chunks:
                    mm_ = pe.matmul(bank[:, :], ws[:, kt, 128 * g:128 * g + 128], xT_s[:, kt, 512 * c:512 * c + 512],
                                    start=(kt == 0), stop=(kt == KT - 1))
                if chunks[-1] == KT - 1:
                    mm_.then_inc(proj_ready, 1)

            def max_item(b, q, m):
                i, qb, c = m // (KB * QC), m // QC % KB, m % QC
                at = MAXES * q + m
                if m == 0:
                    pe.wait_ge(*stacks_there(b, q))
                if at < 2:
                    pe.wait_ge(z_read, b * KB + START)
                pe.wait_ge(mx_done, b * PAIRS * MAXES + max(0, at - 1) + START)
                pe.matmul(mx[at % 2][:, :], qS[0:3 * HD, q % NSTACK, i, 128 * qb:128 * qb + 128],
                          kS[0:3 * HD, q % NSTACK, i, 512 * c:512 * c + 512], start=True, stop=True).then_inc(mx_ready, 1)

            def transpose_max(b, q):
                pe.wait_ge(comb_done, b * 3 * PAIRS + 3 * q + 3 + START)
                if q == 0:
                    pe.wait_ge(v_done, b * KB + KB + START)
                else:
                    pe.wait_ge(mrow_done, b * PAIRS + q + START)
                    if q - 1 in QK_SLOTS:
                        pe.wait_ge(lo_done, b * 4 * QUADS + 4 * QK_SLOTS[q - 1] + 4 + START)
                pe.transpose(w[0:32, 0:128], nm[:, :, :].rearrange("p a c -> p (a c)").bitcast(f32),
                             ident[:, :]).then_inc(mt_ready, 1)

            def scores(b, p, k):
                kb, i = unit_kb_head(k)
                if k == 0:
                    pe.wait_ge(*stacks_there(b, p))
                    pe.wait_ge(m_loaded, (b * PAIRS + p + 1) * 32)
                for c in range(QC):
                    u = 2 * (UNITS * p + k) + c
                    if u < NSC:
                        pe.wait_ge((o_read, yT_done, hm_done)[u], b * KB + START)
                    else:
                        pe.wait_ge(exp_done, b * PAIRS * 2 * UNITS + u - NSC + 1 + START)
                    pe.matmul(sc[u % NSC][:, :], kS[0:KS, p % NSTACK, i, 128 * kb:128 * kb + 128],
                              qS[0:KS, p % NSTACK, i, 512 * c:512 * c + 512], start=True, stop=True).then_inc(sc_ready, 1)

            def out_block(b, p, kb):
                pe.wait_ge(exp_done, b * PAIRS * 2 * UNITS + 2 * (UNITS * p + 2 * kb + 1) + 2 + START)
                if kb == 0:
                    if p == 0:
                        pe.wait_ge(v_done, b * KB + KB + START)
                    else:
                        pe.wait_ge(pv_copied, b * PAIRS + p + START)
                for c in range(QC):
                    for i in range(2):
                        at = HD * (2 * c + i)
                        h = 2 * p + i
                        mm_ = pe.matmul(pv[at:at + HD, :], V[:, kb, HD * h:HD * h + HD],
                                        P[:, (UNITS * p + 2 * kb + i) % NP, 512 * c:512 * c + 512],
                                        start=(kb == 0), stop=(kb == KB - 1))
                mm_.then_inc(pv_done, 1)

            def denominators(b, p, j):
                g = 4 * p + j
                pe.wait_ge(psum_done, b * 8 * PAIRS + 2 * g + 2 + START)
                if j == 0:
                    pe.wait_ge(rden_done, (b * PAIRS + p) * 4 + START)
                for c in range(QC):
                    for i in range(2):
                        at = HD * (2 * c + i)
                        mm_ = pe.matmul(den[at:at + HD, :], ones[:, :], Psum[:, g % 2, i, 512 * c:512 * c + 512],
                                        start=(j == 0), stop=(j == 3))
                mm_.then_inc(den_done, 1)

            start(pe, proj_ready, mx_ready, mt_ready, sc_ready, pv_done, den_done, o_ready, t1_ready, h_ready,
                  t2_ready, z_ready)
            pe.wait_ge(const_ready, 6 + E)
            pe.wait_ge(w_loaded["wq"], 16)
            pe.wait_ge(w_loaded["wk"], 16)
            with pe.Fori(0, B) as b:
                pe.wait_ge(x_loaded, 16 * b + 16)
                pe.wait_ge(hmT_done, b * KB + START)
                pe.wait_ge(hm_done, b * KB + START)
                for g in range(2):
                    for n in range(4):
                        if 4 * g + n >= 2:
                            pe.wait_ge(lo_done, b * 4 * QUADS + 4 * g + n - 1 + START)
                        qk_group(b, g, n, range(KT))
                pe.wait_ge(w_loaded["wv"], 16)
                for t in range(KB):
                    if t < 2:
                        pe.wait_ge(lo_done, b * 4 * QUADS + 7 + t + START)
                    else:
                        pe.wait_ge(v_done, b * KB + t - 1 + START)
                    for kt in range(KT):
                        mm_ = pe.matmul((w, pv)[t % 2][:, :], xT_s[:, kt, 128 * t:128 * t + 128], wv_s[:, kt, :],
                                        start=(kt == 0), stop=(kt == KT - 1))
                    mm_.then_inc(proj_ready, 1)
                    for m in range(5 * t, 5 * t + 5):
                        max_item(b, m // MAXES, m % MAXES)
                transpose_max(b, 0)
                for p in range(PAIRS):
                    for k in range(UNITS):
                        scores(b, p, k)
                        for q, m in max_items(p, k):
                            max_item(b, q, m)
                        if p in QK_SLOTS and proj_pieces(k):
                            n, chunks = proj_pieces(k)
                            if chunks[0] == 0:
                                if n == 0:
                                    pe.wait_ge(mrow_done, b * PAIRS + p + 1 + START)
                                else:
                                    pe.wait_ge(lo_done, b * 4 * QUADS + 4 * QK_SLOTS[p] + n + START)
                            qk_group(b, QK_SLOTS[p], n, chunks)
                        if k == 14 and p + 1 < PAIRS:
                            transpose_max(b, p + 1)
                        if k == 1 and p > 0:
                            out_block(b, p - 1, KB - 1)
                        if k % 2 == 1 and k >= 3:
                            out_block(b, p, (k - 3) // 2)
                        if k in (1, 5) and p > 0:
                            denominators(b, p - 1, 2 + k // 4)
                        if k in (9, 13):
                            denominators(b, p, (k - 9) // 4)
                out_block(b, PAIRS - 1, KB - 1)
                denominators(b, PAIRS - 1, 2)
                denominators(b, PAIRS - 1, 3)

                pe.wait_ge(w_loaded["tail_w"], 16 * 5)
                pe.wait_ge(norm_done, b * 2 * PAIRS + 2 * PAIRS + START)
                pe.wait_ge(exp_done, (b + 1) * PAIRS * 2 * UNITS + START)
                pe.wait_ge(mx_done, (b + 1) * PAIRS * MAXES + START)
                for t in range(KB + 2):
                    if t < KB:
                        pe.wait_ge(o_read, b * KB + t + START)
                        for kt in range(KT):
                            mm_ = pe.matmul(o_ps[:, :], attT[:, kt, 128 * t:128 * t + 128], wo_s[:, kt, :],
                                            start=(kt == 0), stop=(kt == KT - 1))
                        mm_.then_inc(o_ready, 1)
                    if 1 <= t <= KB:
                        pe.wait_ge(yT_done, b * KB + t + START)
                        pe.wait_ge(hm_done, b * KB + t - 1 + START)
                        for kt in range(KT):
                            pe.matmul(l_ps[:, 0:E], yT[:, 128 * kt:128 * kt + 128], wr_s[:, kt, :],
                                      start=(kt == 0), stop=False)
                        pe.matmul(l_ps[:, 0:E], ones_row[:, :], br_s[:, :], start=False, stop=True)
                        for kt in range(KT):
                            mm_ = pe.matmul(h_ps[:, :], yT[:, 128 * kt:128 * kt + 128], a_s[:, kt, :],
                                            start=(kt == 0), stop=(kt == KT - 1))
                        mm_.then_inc(h_ready, 1)
                    if t < KB:
                        pe.wait_ge(y_done, b * KB + t + 1 + START)
                        for kt in range(KT):
                            mm_ = pe.transpose(t1_ps[:, 128 * kt:128 * kt + 128], y[t % 3][:, 128 * kt:128 * kt + 128],
                                               ident[:, :])
                        mm_.then_inc(t1_ready, 1)
                    if t >= 2:
                        pe.wait_ge(hmT_done, b * KB + t - 1 + START)
                        pe.wait_ge(z_read, b * KB + t - 2 + START)
                        for kt in range(KT):
                            mm_ = pe.matmul(z_ps[:, :], hmT[:, 128 * kt:128 * kt + 128], b_s[:, kt, :],
                                            start=(kt == 0), stop=(kt == KT - 1))
                        mm_.then_inc(z_ready, 1)
                    if 1 <= t <= KB:
                        pe.wait_ge(hm_done, b * KB + t + START)
                        for kt in range(KT):
                            mm_ = pe.transpose(t2_ps[:, 128 * kt:128 * kt + 128], hm[:, 128 * kt:128 * kt + 128],
                                               ident[:, :])
                        mm_.then_inc(t2_ready, 1)

        @block.scalar
        def _(act):
            start(act, hi_done, v_done, mrow_done, exp_done, pv_copied, yT_done, lexp_done, hmT_done)
            act.dma_start(wq_s[:, :, :], wqT.rearrange("(k p) n -> p k n", p=128)).then_inc(w_loaded["wq"], 16)

            def hi_part(b, g, n):
                at = (4 * g + n) if g < 2 else (4 * g + n + KB)
                bank = (w, pv)[at % 2] if g < 2 else w
                act.wait_ge(proj_ready, b * NPROJ + at + 1 + START)
                if n == 0:
                    if g > 0:
                        for q in (2 * g - 2, 2 * g - 1):
                            act.wait_ge(*stacks_there(b, q))
                act.activation(nat[("q_hi", "k_hi")[n // 2]][:, 512 * (n % 2):512 * (n % 2) + 512], bank[:, :],
                               ACT.Copy).then_inc(hi_done, 1)

            def copy_max(b, q):
                act.wait_ge(mt_ready, b * PAIRS + q + 1 + START)
                if q > 0:
                    act.wait_ge(m_loaded, (b * PAIRS + q) * 32)
                act.activation(mrow[:, :], w[0:32, 0:128], ACT.Copy).then_inc(mrow_done, 1)

            def copy_out(b, p):
                act.wait_ge(pv_done, b * PAIRS * KB + KB * p + KB + START)
                act.wait_ge(norm_done, (b * PAIRS + p) * 2 + START)
                act.activation(pv_s[:, :], pv[:, :], ACT.Copy).then_inc(pv_copied, 1)

            with act.Fori(0, B) as b:
                for g in range(2):
                    for n in range(4):
                        hi_part(b, g, n)
                act.wait_ge(pv_done, b * PAIRS * KB + START)
                for t in range(KB):
                    act.wait_ge(proj_ready, b * NPROJ + 8 + t + 1 + START)
                    act.activation(V[:, t, :], (w, pv)[t % 2][:, :], ACT.Copy).then_inc(v_done, 1)
                copy_max(b, 0)
                act.wait_ge(tail_stored, b + START)
                for p in range(PAIRS):
                    for k in range(UNITS):
                        unit = UNITS * p + k
                        if unit >= NP:
                            act.wait_ge(pv_done, b * PAIRS * KB + (unit - NP) // 2 + 1 + START)
                            act.wait_ge(psum_done, b * 8 * PAIRS + pool_sums_until(unit - NP) + START)
                        for c in range(QC):
                            u = 2 * unit + c
                            act.wait_ge(sc_ready, b * PAIRS * 2 * UNITS + u + 1 + START)
                            act.activation(P[:, unit % NP, 512 * c:512 * c + 512], sc[u % NSC][:, :],
                                           ACT.Exp).then_inc(exp_done, 1)
                        if k == 2 and p > 0:
                            copy_out(b, p - 1)
                        if p in QK_SLOTS and k in (3, 6, 9, 12):
                            hi_part(b, QK_SLOTS[p], k // 3 - 1)
                        if k == 15 and p + 1 < PAIRS:
                            copy_max(b, p + 1)
                copy_out(b, PAIRS - 1)
                for t in range(KB + 1):
                    if t >= 1:
                        act.wait_ge(nlmax_done, b * KB + t + START)
                        act.activation(lexp[:, :], l_ps[:, 0:E], ACT.Exp, bias=nlmax[:, :],
                                       accum_out=lsum[:, :]).then_inc(lexp_done, 1)
                    if t < KB:
                        act.wait_ge(t1_ready, b * KB + t + 1 + START)
                        act.wait_ge(h_ready, b * KB + t + START)
                        act.activation(yT, t1_ps[:, :], ACT.Copy).then_inc(yT_done, 1)
                    if t >= 1:
                        act.wait_ge(t2_ready, b * KB + t + START)
                        act.wait_ge(z_ready, b * KB + t - 1 + START)
                        act.activation(hmT, t2_ps[:, :], ACT.Copy).then_inc(hmT_done, 1)

        @block.vector
        def _(dve):
            def lo_part(b, g, n):
                at = (4 * g + n) if g < 2 else (4 * g + n + KB)
                bank = (w, pv)[at % 2] if g < 2 else w
                hi, lo = (("q_hi", "q_lo"), ("k_hi", "k_lo"))[n // 2]
                cols = slice(512 * (n % 2), 512 * (n % 2) + 512)
                dve.wait_ge(hi_done, b * 4 * QUADS + 4 * g + n + 1 + START)
                dve.tensor_tensor(nat[lo][:, cols], bank[:, :], nat[hi][:, cols].bitcast(f32),
                                  ALU.subtract).then_inc(lo_done, 1)

            def max_item(b, q, m):
                at = MAXES * q + m
                dve.wait_ge(mx_ready, b * PAIRS * MAXES + at + 1 + START)
                dve.tensor_reduce(mxc[:, q % 2, m:m + 1], mx[at % 2][:, :], AX.X, ALU.max).then_inc(mx_done, 1)
                if m == MAXES - 1:
                    n = b * 3 * PAIRS + 3 * q
                    dve.wait_ge(mx_done, b * PAIRS * MAXES + at + 1 + START)
                    dve.tensor_reduce(mm[:, :], mxc[:, q % 2, :].rearrange("p (a c) -> p a c", c=QC), AX.X,
                                      ALU.max).then_inc(comb_done, 1)
                    dve.wait_ge(mt_ready, b * PAIRS + q + START)
                    dve.wait_ge(comb_done, n + 1 + START)
                    dve.tensor_scalar(nm[:, 0, :], mm[:, :], -1.0, None, ALU.mult).then_inc(comb_done, 1)
                    dve.wait_ge(comb_done, n + 2 + START)
                    dve.scalar_tensor_tensor(out=nm[:, 1, :], in0=mm[:, :], scalar=-1.0, in1=nm[:, 0, :].bitcast(f32),
                                             op0=ALU.mult, op1=ALU.subtract).then_inc(comb_done, 1)

            def reciprocal_piece(b, p, n):
                dve.wait_ge(den_done, b * 4 * PAIRS + 4 * p + 4 + START)
                if n == 0:
                    dve.wait_ge(norm_done, (b * PAIRS + p) * 2 + START)
                dve.reciprocal(rden[:, 128 * n:128 * n + 128], den[:, 128 * n:128 * n + 128]).then_inc(rden_done, 1)

            def normalise(b, p):
                dve.wait_ge(rden_done, (b * PAIRS + p) * 4 + 4 + START)
                dve.wait_ge(pv_copied, b * PAIRS + p + 1 + START)
                if p == 0:
                    dve.wait_ge(o_ready, b * KB + START)
                for c in range(QC):
                    dve.tensor_tensor(attT[64 * (p % 2):64 * (p % 2) + 64, p // 2, 512 * c:512 * c + 512],
                                      pv_s[64 * c:64 * c + 64, :], rden[64 * c:64 * c + 64, :],
                                      ALU.mult).then_inc(norm_done, 1)

            start(dve, lo_done, mx_done, comb_done, rden_done, norm_done, o_read, stat1, y_done, nlmax_done, hm_done,
                  z_read, stat2, out_done, tail_step)
            dve.memset(kS[3 * HD:KS, :, :, :].bitcast(f32), 1.0).then_inc(const_ready, 1)
            dve.wait_ge(const_ready, 6 + E)
            with dve.Fori(0, B) as b:
                for g in range(2):
                    for n in range(4):
                        lo_part(b, g, n)
                for m in range(5 * KB):
                    max_item(b, m // MAXES, m % MAXES)
                for p in range(PAIRS):
                    for k in range(UNITS):
                        for q, m in max_items(p, k):
                            max_item(b, q, m)
                        if p in QK_SLOTS and k in (3, 6, 9, 12):
                            lo_part(b, QK_SLOTS[p], k // 3 - 1)
                        if p > 0 and 5 <= k < 9:
                            reciprocal_piece(b, p - 1, k - 5)
                        if p > 0 and k == 9:
                            normalise(b, p - 1)
                for n in range(4):
                    reciprocal_piece(b, PAIRS - 1, n)
                normalise(b, PAIRS - 1)

                step = 0

                def did(ins):
                    nonlocal step
                    step += 1
                    ins.then_inc(tail_step, 1)

                def last():
                    dve.wait_ge(tail_step, b * TAIL_STEPS + step + START)

                for t in range(KB + 2):
                    if t < KB:
                        dve.wait_ge(o_ready, b * KB + t + 1 + START)
                        dve.wait_ge(xt_loaded[t % 2], (b * (KB // 2) + t // 2 + 1) * 16)
                        dve.tensor_tensor(xt[t % 2], o_ps[:, :], xt[t % 2], ALU.add).then_inc(o_read, 1)
                        dve.wait_ge(o_read, b * KB + t + 1 + START)
                        did(dve.bn_stats(st1[:, :], xt[t % 2]))
                        dve.wait_ge(y_done, b * KB + t + START)
                        last()
                        dve.memset(settle[:, :], 0.0)
                        dve.bn_aggr(mv1[:, :], st1[:, :]).then_inc(stat1, 1)
                    if 1 <= t <= KB:
                        dve.wait_ge(h_ready, b * KB + t + START)
                        did(dve.tensor_reduce(lmax[:, :], l_ps[:, 0:E], AX.X, ALU.max))
                        last()
                        dve.wait_ge(lexp_done, b * KB + t - 1 + START)
                        dve.tensor_scalar(nlmax[:, :], lmax[:, :], -1.0, None, ALU.mult).then_inc(nlmax_done, 1)
                    if t < KB:
                        dve.wait_ge(rstd1, b * KB + t + 1 + START)
                        dve.tensor_scalar(y[t % 3], xt[t % 2], mv1[:, 0:1], rs1[:, :], ALU.subtract,
                                          ALU.mult).then_inc(y_done, 1)
                    if 1 <= t <= KB:
                        dve.wait_ge(lexp_done, b * KB + t + START)
                        did(dve.reciprocal(lrec[:, :], lsum[:, :]))
                        did(dve.scalar_tensor_tensor(out=eq[:, :], in0=l_ps[:, 0:E], scalar=lmax[:, :], in1=rank[:, :],
                                                     op0=ALU.is_ge, op1=ALU.mult))
                        last()
                        did(dve.tensor_reduce(eqm[:, :], eq[:, :], AX.X, ALU.max))
                        last()
                        did(dve.tensor_scalar(gate[:, :], eq[:, :], eqm[:, :], lrec[:, :], ALU.is_equal, ALU.mult))
                        last()
                        if t >= 2:
                            dve.wait_ge(t2_ready, b * KB + t - 1 + START)
                        dve.scalar_tensor_tensor(out=hm.rearrange("p (e r) -> p e r", e=E),
                                                 in0=h_ps[:, :].rearrange("p (e r) -> p e r", e=E), scalar=SCALING,
                                                 in1=gate[:, :].unsqueeze(2).to_broadcast([128, E, R]),
                                                 op0=ALU.mult, op1=ALU.mult).then_inc(hm_done, 1)
                    if t >= 2:
                        dve.wait_ge(z_ready, b * KB + t - 1 + START)
                        if t >= 4:
                            dve.wait_ge(out_stored[t % 2], (b * (KB // 2) + (t - 2) // 2) * 16)
                        dve.tensor_tensor(z_s[t % 2], z_ps[:, :], y[(t - 2) % 3], ALU.add).then_inc(z_read, 1)
                        dve.wait_ge(z_read, b * KB + t - 1 + START)
                        did(dve.bn_stats(st2[:, :], z_s[t % 2]))
                        last()
                        dve.memset(settle[:, :], 0.0)
                        dve.bn_aggr(mv2[:, :], st2[:, :]).then_inc(stat2, 1)
                        dve.wait_ge(rstd2, b * KB + t - 1 + START)
                        dve.tensor_scalar(z_s[t % 2], z_s[t % 2], mv2[:, 0:1], rs2[:, :], ALU.subtract,
                                          ALU.mult).then_inc(out_done, 1)
                assert step == TAIL_STEPS


TAIL_STEPS = 8 * 7


def kernel(L0_attn_x, L0_attn_wq, L0_attn_wk, L0_attn_wv, L0_attn_wo, L0_ffn_A, L0_ffn_B, L0_ffn_Wr, L0_ffn_br):
    import numpy as np
    import concourse.bacc as bacc
    from concourse.bass_utils import run_bass_kernel_spmd

    x = np.asarray(L0_attn_x)
    d = x.shape[-1]
    e, r = L0_ffn_A.shape[:2]
    arrays = {
        "xT": np.ascontiguousarray(x.reshape(-1, d).T),
        "x": np.ascontiguousarray(x),
        "wqT": np.ascontiguousarray(np.asarray(L0_attn_wq).T),
        "wkT": np.ascontiguousarray(np.asarray(L0_attn_wk).T),
        "wvT": np.ascontiguousarray(np.asarray(L0_attn_wv).T),
        "woT": np.ascontiguousarray(np.asarray(L0_attn_wo).T),
        "aT": np.ascontiguousarray(np.asarray(L0_ffn_A).reshape(e * r, d).T),
        "bT": np.ascontiguousarray(np.asarray(L0_ffn_B).transpose(0, 2, 1).reshape(e * r, d)),
        "wrT": np.ascontiguousarray(np.asarray(L0_ffn_Wr).T),
        "br": np.ascontiguousarray(np.asarray(L0_ffn_br).reshape(1, e)),
    }
    nc = bacc.Bacc("TRN2", target_bir_lowering=False, num_devices=1)
    args = [nc.dram_tensor(n, a.shape, mybir.dt.from_np(a.dtype), kind="ExternalInput").ap() for n, a in arrays.items()]
    out = nc.dram_tensor("out", x.shape, mybir.dt.float32, kind="ExternalOutput").ap()
    build_attention_lora_moe_block(nc, *args, out)
    result = run_bass_kernel_spmd(nc, [arrays], core_ids=[0])
    return result.results[0]["out"]
```

```python
from contextlib import ExitStack

import concourse.bass as bass
from concourse import mybir


class Batch:

    def __init__(self, loop, offset=0):
        self.loop, self.offset = loop, offset
        self.first = type(loop) is int and loop + offset == 0

    def __add__(self, n):
        return Batch(self.loop, self.offset + n)

    def __sub__(self, n):
        return Batch(self.loop, self.offset - n)

    def count(self, a_batch, n):
        return self.loop * a_batch + (self.offset * a_batch + n)


def build_attention_lora_moe_block(nc, xT, x, wqT, wkT, wvT, woT, aT, bT, wrT, br, out):
    f32, f32r = mybir.dt.float32, mybir.dt.float32r
    ALU, ACT, AX = mybir.AluOpType, mybir.ActivationFunctionType, mybir.AxisListType

    D, TOK = xT.shape
    B, S, _ = x.shape
    E = br.shape[1]
    R = aT.shape[1] // E
    HD = 32
    H = D // HD
    KT = D // 128
    QC = S // 512
    KB = S // 128
    PAIRS = H // 2
    QUADS = H // 4
    UNITS = 2 * KB
    SCORES = UNITS * QC
    MAXES = 2 * KB * QC
    ADDS = UNITS - 2
    KS = 3 * HD + 2
    NP, NSC, NMX = 6, 2, 3
    HALF = KB // 2
    START = 1
    EPS, SCALING = 1e-5, 1.0 / R
    STACK_INCS = 6 * 16
    K_HI, K_LO, Q_HI, Q_LO = range(4)

    first, final = Batch(0), Batch(B - 1)
    ctx = ExitStack()
    with ctx:
        def sb(name, shape, dt=f32):
            return ctx.enter_context(nc.sbuf_tensor(name, shape, dt))

        def ps(name, shape):
            return ctx.enter_context(nc.psum_tensor(name, shape, f32))

        def sem(name):
            return ctx.enter_context(nc.semaphore(name))

        wq_s, wk_s, wv_s, wo_s = (sb(n, [128, KT, D]) for n in ("wq_s", "wk_s", "wv_s", "wo_s"))
        a_s, b_s = sb("a_s", [128, KT, E * R]), sb("b_s", [128, KT, D])
        wr_s, br_s = sb("wr_s", [128, KT, E]), sb("br_s", [1, E])
        xT_s = sb("xT_s", [128, KT, S])
        parts = sb("parts", [128, 4, S], f32r)
        stacks = sb("stacks", [128, 2, 2, 2, S], f32r)
        V = sb("V", [128, KB, D])
        P = sb("P", [128, NP, S])
        Psum = sb("Psum", [128, 2, S])
        attT = sb("attT", [128, KT, S])
        pv_s, rden = sb("pv_s", [128, 512]), sb("rden", [128, 512])
        r = sb("r", [128, KB, D])
        yT, hm, hmT = sb("yT", [128, D]), sb("hm", [128, E * R]), sb("hmT", [128, E * R])
        mxc = sb("mxc", [128, 2, MAXES])
        mm = sb("mm", [128, 2 * KB])
        nm = sb("nm", [128, 2, 2 * KB], f32r)
        mrow = sb("mrow", [32, 128], f32r)
        ident, ones, ones_row = sb("ident", [128, 128]), sb("ones", [128, 32]), sb("ones_row", [1, 128])
        rank = sb("rank", [128, E])
        mhalf, eps_s, settle = sb("mhalf", [128, HALF]), sb("eps_s", [128, HALF]), sb("settle", [128, 1])
        stats, mv = sb("stats", [128, KB, 6]), sb("mv", [128, KB, 2])
        ve, rstd = sb("ve", [128, HALF]), sb("rstd", [128, KB])
        lmax, nlmax = sb("lmax", [128, 1]), sb("nlmax", [128, 1])
        lexp, lsum, lrec = sb("lexp", [128, E]), sb("lsum", [128, 1]), sb("lrec", [128, 1])
        eq, eqm, gate = sb("eq", [128, E]), sb("eqm", [128, 1]), sb("gate", [128, E])

        sc = [ps(f"sc{i}", [128, 512]) for i in range(NSC)]
        mx = [ps(f"mx{i}", [128, 512]) for i in range(NMX)]
        pv, den, w = ps("pv", [128, 512]), ps("den", [128, 512]), ps("w", [128, 512])

        const_ready, ident_zero, x_loaded = sem("const_ready"), sem("ident_zero"), sem("x_loaded")
        w_loaded = {n: sem(f"{n}_loaded") for n in ("wq", "wk", "wv", "tail_w")}
        qk_ready, hi_done, lo_done = sem("qk_ready"), sem("hi_done"), sem("lo_done")
        v_ready, v_done = sem("v_ready"), sem("v_done")
        stack_free, stack_loaded = sem("stack_free"), [sem(f"stack_loaded{i}") for i in range(2)]
        m_loaded = sem("m_loaded")
        mx_ready, mx_done, comb_done = sem("mx_ready"), sem("mx_done"), sem("comb_done")
        mt_ready, mrow_done = sem("mt_ready"), sem("mrow_done")
        sc_ready, exp_done, pv_done, pv_copied = sem("sc_ready"), sem("exp_done"), sem("pv_done"), sem("pv_copied")
        add_done, den_done, den_copied = sem("add_done"), sem("den_done"), sem("den_copied")
        rden_done, norm_done = sem("rden_done"), sem("norm_done")
        r_loaded, o_ready, o_read = sem("r_loaded"), sem("o_ready"), sem("o_read")
        stats_done, mv_done, ve_done, rstd_done = sem("stats_done"), sem("mv_done"), sem("ve_done"), sem("rstd_done")
        y_done, t1_ready, yT_done, h_ready = sem("y_done"), sem("t1_ready"), sem("yT_done"), sem("h_ready")
        nlmax_done, lexp_done, gate_step, hm_done = sem("nlmax_done"), sem("lexp_done"), sem("gate_step"), sem("hm_done")
        t2_ready, hmT_done, z_ready, z_read = sem("t2_ready"), sem("hmT_done"), sem("z_ready"), sem("z_read")
        out_done, out_stored = sem("out_done"), [sem(f"out_stored{i}") for i in range(2)]

        MAX_FIRST, MAX_STEP, MAX_T = 3, 3, 14
        DEN_AT, REC_AT, NORM_AT = 3, 4, 8
        QK_SLOTS = {0: 1, 2: 2, 4: 3, 6: 0}

        def tail_pieces():
            pieces = []
            for t in range(KB):
                pieces += [("t1", t), ("h", t)] + ([("z", t - 1)] if t else []) + [("t2", t)]
            return pieces + [("z", KB - 1)]

        def plan(tail, v_there):
            at = {(p, MAX_T): ("max_t", None) for p in range(PAIRS)}
            for p in QK_SLOTS:
                for n in range(4):
                    at[p, 4 + n] = ("qk", n)
            for kb, k in enumerate((4, 6, 8, 10, 12, 15)):
                at[7, k] = ("v", kb)
            if not v_there:
                at[0, 0], at[0, 2] = ("v", 6), ("v", 7)
            if tail:
                for t, spot in enumerate([(0, k) for k in (9, 10, 11, 12, 13, 15)] + [(1, 0), (1, 1)]):
                    at[spot] = ("o", t)
                spots = [(p, k) for p in range(1, 4) for k in range(UNITS) if (p, k) > (1, 1) and (p, k) not in at]
                for spot, piece in zip(spots, tail_pieces()):
                    at[spot] = piece
            return at

        PLAN = {flags: plan(*flags) for flags in ((True, False), (False, True))}
        LN_STATS = {(0, 13): (0, 0), (1, 2): (0, 1), (2, 9): (1, 0), (3, 8): (1, 1)}
        LN_APPLY = {(0, 15): (0, 0), (1, 4): (0, 1), (2, 11): (1, 0), (3, 10): (1, 1)}

        def after(b, p):
            return (b, p + 1) if p + 1 < PAIRS else (b + 1, 0)

        def before(b, p):
            return (b, p - 1) if p else (b - 1, PAIRS - 1)

        def max_items(k):
            m = (k - MAX_FIRST) * MAX_STEP
            return range(m, min(m + MAX_STEP, MAXES)) if m >= 0 else ()

        def stacks_there(b, q):
            return stack_loaded[q % 2], b.count(PAIRS // 2 * STACK_INCS, (q // 2 + 1) * STACK_INCS)

        def adds_until(unit):
            p, k = divmod(unit, UNITS)
            return ADDS * p + (k + 1 if k < 2 else k - 1)

        CONSTS = 3 + 3 + E
        GATE_STEPS = 4 + 1
        LAST_BANK = {"t1": mx[0], "h": mx[2], "t2": mx[1], "z": sc[1]}

        def o_bank(t):
            return (w, sc[0])[t % 2]

        def rotate(count, buffers, shifted):
            at = [n % buffers for n in range(count)]
            at[count - len(shifted):] = shifted
            twice = at + at
            return at, [max(m for m in range(count + n) if twice[m] == at[n]) - count for n in range(count)]

        BUFFER, BUFFER_BEFORE = rotate(PAIRS * UNITS, NP, [2, 3])
        BANK, BANK_BEFORE = rotate(PAIRS * SCORES, NSC, [])
        MAX_BANK, MAX_BANK_BEFORE = rotate(PAIRS * MAXES, NMX, [1])


        def fresh(engine, loop):
            copy = engine.alloc_register()
            engine.reg_mov(copy, loop)
            return engine.snap(copy, donate=True)

        def start(engine, *semaphores):
            for s in semaphores:
                engine.sem_inc(s, START)

        block = ctx.enter_context(nc.Block())

        @block.sync
        def _(sp):
            xT_v = xT.rearrange("(k p) t -> p k t", p=128)

            def load_stacks(b, q):
                sp.wait_ge(stack_free, b.count(PAIRS, q + 1 + START))
                for n, (k_part, q_part) in enumerate(((K_HI, Q_HI), (K_LO, Q_HI), (K_HI, Q_LO))):
                    for i in range(2):
                        row = 2 * HD * (q % 2) + HD * i
                        sp.dma_start(stacks[HD * n:HD * n + HD, q % 2, :, i, :].bitcast(f32),
                                     parts[row:row + HD, k_part:q_part + 1:q_part - k_part, :].bitcast(f32)) \
                            .then_inc(stack_loaded[q % 2], 16)

            def load_max(b, q):
                sp.wait_ge(mrow_done, b.count(PAIRS, q + 1 + START))
                for n in range(2):
                    sp.dma_start(stacks[3 * HD + n:3 * HD + n + 1, q % 2, 1, :, :].bitcast(f32)
                                 .rearrange("a i (r t) -> a (i r) t", t=128),
                                 mrow[16 * n:16 * n + 16, :].bitcast(f32)).then_inc(m_loaded, 16)

            def rows(tensor, b, t, n):
                return tensor.rearrange("b s d -> (b s) d")[bass.ds(b.count(S, 128 * t), 128 * n), :] \
                    .rearrange("(t p) d -> p t d", p=128)

            def store(b, half):
                sp.wait_ge(out_done, b.count(KB, HALF * (half + 1) + START))
                sp.dma_start(rows(out, b, HALF * half, HALF), r[:, HALF * half:HALF * half + HALF, :]) \
                    .then_inc(out_stored[half], 16)

            def slot(b, p, tail, more):
                if more or p + 1 < PAIRS:
                    load_stacks(*after(b, p))
                if p == 5 and more:
                    sp.wait_ge(qk_ready, b.count(4 * QUADS, 4 * QUADS + START))
                    sp.dma_start(xT_s[:, :, :], xT_v[:, :, bass.ds(b.count(S, S), S)]).then_inc(x_loaded, 16)
                if p == 7:
                    for stored in out_stored:
                        sp.wait_ge(stored, b.count(16, 16))
                    sp.dma_start(r[:, :, :], rows(x, b, 0, KB)).then_inc(r_loaded, 16)
                if more or p + 1 < PAIRS:
                    load_max(*after(b, p))
                if p == 3 and tail:
                    store(b - 1, 0)
                    store(b - 1, 1)

            for stored in out_stored:
                sp.sem_inc(stored, 16)
            sp.dma_start(xT_s[:, :, :], xT_v[:, :, 0:S]).then_inc(x_loaded, 16)
            load_stacks(first, 0)
            load_max(first, 0)
            for p in range(4):
                slot(first, p, False, True)
            with sp.Fori(0, B - 1) as i:
                b = Batch(i)
                for p in range(4, 8):
                    slot(Batch(fresh(sp, i)), p, True, True)
                for p in range(4):
                    slot(Batch(fresh(sp, i), 1), p, True, True)
            for p in range(4, 8):
                slot(final, p, True, False)
            store(final, 0)
            store(final, 1)
            for stored in out_stored:
                sp.wait_ge(stored, B * 16 + 16)

        @block.gpsimd
        def _(pool):
            start(pool, add_done, ve_done, rstd_done)
            pool.dma_start(wk_s[:, :, :], wkT.rearrange("(k p) n -> p k n", p=128)).then_inc(w_loaded["wk"], 16)
            pool.dma_start(wv_s[:, :, :], wvT.rearrange("(k p) n -> p k n", p=128)).then_inc(w_loaded["wv"], 16)
            for s, d in ((wo_s, woT), (a_s, aT), (b_s, bT), (wr_s, wrT)):
                pool.dma_start(s[:, :, :], d.rearrange("(k p) n -> p k n", p=128)).then_inc(w_loaded["tail_w"], 16)
            pool.dma_start(br_s[:, :], br).then_inc(w_loaded["tail_w"], 16)
            pool.memset(ident[:, :], 0.0).then_inc(ident_zero, 1)
            pool.wait_ge(ident_zero, 1)
            pool.affine_select(out=ident[:, :], in_=ident[:, :], compare_op=ALU.not_equal, fill=1.0,
                               base=0, pattern=[[-1, 128]], channel_multiplier=1).then_inc(const_ready, 1)
            pool.memset(mhalf[:, :], -0.5).then_inc(const_ready, 1)
            pool.memset(eps_s[:, :], EPS).then_inc(const_ready, 1)
            pool.wait_ge(const_ready, CONSTS)

            def add(b, p, k):
                unit = UNITS * p + k
                pool.wait_ge(exp_done, b.count(PAIRS * SCORES, QC * (unit + 1) + START))
                if k < 4:
                    pool.wait_ge(den_done, b.count(PAIRS, p + START))
                    so_far = P[:, BUFFER[unit - 2], :]
                else:
                    pool.wait_ge(add_done, b.count(PAIRS * ADDS, ADDS * p + k - 3 + START))
                    so_far = Psum[:, k % 2, :]
                pool.tensor_tensor(Psum[:, k % 2, :], so_far, P[:, BUFFER[unit], :], ALU.add).then_inc(add_done, 1)

            def reciprocal_deviation(b, n, half):
                at = b.count(4, 2 * n + half + 1 + START)
                tiles = slice(HALF * half, HALF * half + HALF)
                pool.wait_ge(mv_done, at)
                pool.tensor_tensor(ve[:, :], mv[:, tiles, 1], eps_s[:, :], ALU.add).then_inc(ve_done, 1)
                pool.wait_ge(ve_done, at)
                pool.tensor_tensor(rstd[:, tiles], ve[:, :], mhalf[:, :], ALU.pow).then_inc(rstd_done, 1)

            def slot(b, p, tail):
                for k in range(UNITS):
                    if k >= 2:
                        add(b, p, k)
                    if tail and (p, k) in LN_STATS:
                        reciprocal_deviation(b - 1, *LN_STATS[p, k])

            for p in range(4):
                slot(first, p, False)
            with pool.Fori(0, B - 1) as i:
                b = Batch(i)
                for p in range(4, 8):
                    slot(Batch(fresh(pool, i)), p, True)
                for p in range(4):
                    slot(Batch(fresh(pool, i), 1), p, True)
            for p in range(4, 8):
                slot(final, p, True)
            for n in range(2):
                for half in range(2):
                    reciprocal_deviation(final, n, half)

        @block.tensor
        def _(pe):
            reader = {}

            def take(bank, semaphore, value):
                if bank.name in reader:
                    pe.wait_ge(*reader[bank.name])
                reader[bank.name] = (semaphore, value + START)

            def qk(b, g, n, bank):
                ws, c = (wq_s, wk_s)[n // 2], n % 2
                if n == 0:
                    pe.wait_ge(x_loaded, b.count(16, 16))
                take(bank, lo_done, b.count(4 * QUADS, 4 * g + n + 1))
                for kt in range(KT):
                    done = pe.matmul(bank[:, :], ws[:, kt, 128 * g:128 * g + 128], xT_s[:, kt, 512 * c:512 * c + 512],
                                     start=(kt == 0), stop=(kt == KT - 1))
                done.then_inc(qk_ready, 1)

            def v(b, kb, bank):
                take(bank, v_done, b.count(KB, kb + 1))
                for kt in range(KT):
                    done = pe.matmul(bank[:, :], xT_s[:, kt, 128 * kb:128 * kb + 128], wv_s[:, kt, :],
                                     start=(kt == 0), stop=(kt == KT - 1))
                done.then_inc(v_ready, 1)

            def max_item(b, q, m):
                i, qb, c = m // (KB * QC), m // QC % KB, m % QC
                at = MAXES * q + m
                if m == 0:
                    pe.wait_ge(*stacks_there(b, q))
                if not (b.first and at < NMX):
                    pe.wait_ge(mx_done, b.count(PAIRS * MAXES, MAX_BANK_BEFORE[at] + 1 + START))
                pe.matmul(mx[MAX_BANK[at]][:, :], stacks[0:3 * HD, q % 2, 1, i, 128 * qb:128 * qb + 128],
                          stacks[0:3 * HD, q % 2, 0, i, 512 * c:512 * c + 512], start=True, stop=True).then_inc(mx_ready, 1)

            def max_t(b, q, bank):
                pe.wait_ge(comb_done, b.count(3 * PAIRS, 3 * q + 3 + START))
                take(bank, mrow_done, b.count(PAIRS, q + 1))
                pe.transpose(bank[0:32, 0:128], nm[:, :, :].rearrange("p a c -> p (a c)").bitcast(f32),
                             ident[:, :]).then_inc(mt_ready, 1)

            def score(b, p, k, c):
                kb, i = k // 2, k % 2
                u = SCORES * p + QC * k + c
                if k == 0 and c == 0:
                    pe.wait_ge(*stacks_there(b, p))
                    pe.wait_ge(m_loaded, b.count(PAIRS * 32, 32 * p + 32))
                if not (b.first and u < NSC):
                    pe.wait_ge(exp_done, b.count(PAIRS * SCORES, BANK_BEFORE[u] + 1 + START))
                pe.matmul(sc[BANK[u]][:, :], stacks[0:KS, p % 2, 0, i, 128 * kb:128 * kb + 128],
                          stacks[0:KS, p % 2, 1, i, 512 * c:512 * c + 512], start=True, stop=True).then_inc(sc_ready, 1)

            def out_block(b, p, kb):
                pe.wait_ge(exp_done, b.count(PAIRS * SCORES, QC * (UNITS * p + 2 * kb + 2) + START))
                if p == 0:
                    pe.wait_ge(v_done, b.count(KB, kb + 1 + START))
                if kb == 0 and not (b.first and p == 0):
                    pe.wait_ge(pv_copied, b.count(PAIRS, p + START))
                for c in range(QC):
                    for i in range(2):
                        at = HD * (2 * c + i)
                        h = 2 * p + i
                        done = pe.matmul(pv[at:at + HD, :], V[:, kb, HD * h:HD * h + HD],
                                         P[:, BUFFER[UNITS * p + 2 * kb + i], 512 * c:512 * c + 512],
                                         start=(kb == 0), stop=(kb == KB - 1))
                done.then_inc(pv_done, 1)

            def denominators(b, p):
                pe.wait_ge(add_done, b.count(PAIRS * ADDS, ADDS * (p + 1) + START))
                if not (b.first and p == 0):
                    pe.wait_ge(den_copied, b.count(PAIRS, p + START))
                take(den, den_copied, b.count(PAIRS, p + 1))
                for c in range(QC):
                    for i in range(2):
                        at = HD * (2 * c + i)
                        done = pe.matmul(den[at:at + HD, :], ones[:, :], Psum[:, i, 512 * c:512 * c + 512],
                                         start=True, stop=True)
                done.then_inc(den_done, 1)

            def o(b, t, bank):
                if t == 0:
                    pe.wait_ge(norm_done, b.count(2 * PAIRS, 2 * PAIRS + START))
                take(bank, o_read, b.count(KB, t + 1))
                for kt in range(KT):
                    done = pe.matmul(bank[:, :], attT[:, kt, 128 * t:128 * t + 128], wo_s[:, kt, :],
                                     start=(kt == 0), stop=(kt == KT - 1))
                done.then_inc(o_ready, 1)

            def t1(b, t, bank):
                take(bank, yT_done, b.count(KB, t + 1))
                pe.wait_ge(y_done, b.count(KB, t + 1 + START))
                for kt in range(KT):
                    done = pe.transpose(bank[:, 128 * kt:128 * kt + 128], r[:, t, 128 * kt:128 * kt + 128], ident[:, :])
                done.then_inc(t1_ready, 1)

            def h(b, t, bank):
                pe.wait_ge(yT_done, b.count(KB, t + 1 + START))
                take(den, hm_done, b.count(KB, t + 1))
                take(bank, hm_done, b.count(KB, t + 1))
                for kt in range(KT):
                    pe.matmul(den[:, 0:E], yT[:, 128 * kt:128 * kt + 128], wr_s[:, kt, :], start=(kt == 0), stop=False)
                pe.matmul(den[:, 0:E], ones_row[:, :], br_s[:, :], start=False, stop=True)
                for kt in range(KT):
                    done = pe.matmul(bank[:, :], yT[:, 128 * kt:128 * kt + 128], a_s[:, kt, :],
                                     start=(kt == 0), stop=(kt == KT - 1))
                done.then_inc(h_ready, 1)

            def t2(b, t, bank):
                take(bank, hmT_done, b.count(KB, t + 1))
                pe.wait_ge(hm_done, b.count(KB, t + 1 + START))
                for kt in range(KT):
                    done = pe.transpose(bank[:, 128 * kt:128 * kt + 128], hm[:, 128 * kt:128 * kt + 128], ident[:, :])
                done.then_inc(t2_ready, 1)

            def z(b, t, bank):
                pe.wait_ge(hmT_done, b.count(KB, t + 1 + START))
                take(bank, z_read, b.count(KB, t + 1))
                for kt in range(KT):
                    done = pe.matmul(bank[:, :], hmT[:, 128 * kt:128 * kt + 128], b_s[:, kt, :],
                                     start=(kt == 0), stop=(kt == KT - 1))
                done.then_inc(z_ready, 1)

            def slot(b, p, tail, v_there, more):
                at = PLAN[tail, v_there]
                for k in range(UNITS):
                    maxima = [(*after(b, p), m) for m in max_items(k)] if more or p + 1 < PAIRS else []
                    score(b, p, k, 0)
                    if maxima:
                        max_item(*maxima[0])
                    score(b, p, k, 1)
                    for item in maxima[1:2]:
                        max_item(*item)
                    if k == 1 and not (v_there and p == 0):
                        out_block(*before(b, p), KB - 1)
                    if k % 2 == 1 and k >= 3:
                        out_block(b, p, (k - 3) // 2)
                    for item in maxima[2:]:
                        max_item(*item)
                    if k == DEN_AT and not (v_there and p == 0):
                        denominators(*before(b, p))
                    kind, n = at.get((p, k), (None, None))
                    if kind == "max_t" and (more or p + 1 < PAIRS):
                        max_t(*after(b, p), w)
                    elif kind == "qk" and (more or p < 6):
                        qk(b + (p == 6), QK_SLOTS[p], n, w)
                    elif kind == "v" and (more or p == 0):
                        v(b + (p == 7), n, w)
                    elif kind in ("o", "t1", "h", "t2", "z"):
                        {"o": o, "t1": t1, "h": h, "t2": t2, "z": z}[kind](b - 1, n, w)

            start(pe, qk_ready, v_ready, mx_ready, mt_ready, sc_ready, pv_done, den_done, o_ready, t1_ready, h_ready,
                  t2_ready, z_ready)
            pe.wait_ge(const_ready, CONSTS)
            pe.wait_ge(w_loaded["wq"], 16)
            pe.wait_ge(w_loaded["wk"], 16)
            for n in range(4):
                qk(first, 0, n, (w, pv)[n % 2])
            pe.wait_ge(w_loaded["wv"], 16)
            for kb in range(KB):
                v(first, kb, (w, pv)[kb % 2])
                for m in range(4 * kb, 4 * kb + 4):
                    max_item(first, 0, m)
            max_t(first, 0, w)
            pe.wait_ge(v_done, KB + START)
            for p in range(4):
                slot(first, p, False, True, True)
            pe.wait_ge(w_loaded["tail_w"], 16 * 5)
            with pe.Fori(0, B - 1) as i:
                b = Batch(i)
                reader[w.name] = (mrow_done, b.count(PAIRS, 5 + START))
                reader[den.name] = (hm_done, b.count(KB, START))
                for p in range(4, 8):
                    slot(Batch(fresh(pe, i)), p, True, False, True)
                for p in range(4):
                    slot(Batch(fresh(pe, i), 1), p, True, False, True)
            reader[w.name] = (mrow_done, final.count(PAIRS, 5 + START))
            reader[den.name] = (hm_done, final.count(KB, START))
            for p in range(4, 8):
                slot(final, p, True, False, False)
            out_block(final, PAIRS - 1, KB - 1)
            denominators(final, PAIRS - 1)
            pe.wait_ge(exp_done, B * PAIRS * SCORES + START)
            pe.wait_ge(mx_done, B * PAIRS * MAXES + START)
            for t in range(KB):
                o(final, t, o_bank(t))
            for kind, t in tail_pieces():
                {"t1": t1, "h": h, "t2": t2, "z": z}[kind](final, t, LAST_BANK[kind])

        @block.scalar
        def _(act):
            start(act, hi_done, v_done, mrow_done, exp_done, pv_copied, den_copied, yT_done, lexp_done, hmT_done, stack_free)
            act.dma_start(wq_s[:, :, :], wqT.rearrange("(k p) n -> p k n", p=128)).then_inc(w_loaded["wq"], 16)

            def hi_part(b, g, n, bank):
                act.wait_ge(qk_ready, b.count(4 * QUADS, 4 * g + n + 1 + START))
                if n == 0 and not (b.first and g == 0):
                    for back in (1, 2):
                        act.wait_ge(*(stacks_there(b, 2 * g - back) if g else stacks_there(b - 1, PAIRS - back)))
                act.activation(parts[:, (Q_HI, K_HI)[n // 2], 512 * (n % 2):512 * (n % 2) + 512], bank[:, :],
                               ACT.Copy).then_inc(hi_done, 1)

            def copy_v(b, kb, bank):
                act.wait_ge(v_ready, b.count(KB, kb + 1 + START))
                if not (b.first):
                    act.wait_ge(pv_done, b.count(PAIRS * KB, -KB + kb + 1 + START))
                act.activation(V[:, kb, :], bank[:, :], ACT.Copy).then_inc(v_done, 1)

            def copy_max(b, q, bank):
                act.wait_ge(mt_ready, b.count(PAIRS, q + 1 + START))
                if not (b.first and q == 0):
                    act.wait_ge(m_loaded, b.count(PAIRS * 32, 32 * q))
                act.activation(mrow[:, :], bank[0:32, 0:128], ACT.Copy).then_inc(mrow_done, 1)

            def copy_out(b, p):
                act.wait_ge(pv_done, b.count(PAIRS * KB, KB * p + KB + START))
                act.wait_ge(norm_done, b.count(PAIRS * 2, 2 * p + START))
                act.activation(pv_s[:, :], pv[:, :], ACT.Copy).then_inc(pv_copied, 1)

            def copy_denominators(b, p):
                act.wait_ge(den_done, b.count(PAIRS, p + 1 + START))
                act.wait_ge(norm_done, b.count(PAIRS * 2, 2 * p + START))
                act.activation(rden[:, :], den[:, :], ACT.Copy).then_inc(den_copied, 1)

            def free_stacks(b, q):
                act.wait_ge(lo_done, b.count(4 * QUADS, 4 * (q // 2) + 4 + START))
                act.sem_inc(stack_free, 1)

            def exp(b, p, k):
                unit = UNITS * p + k
                if not (b.first and unit < NP):
                    last, last_b = BUFFER_BEFORE[unit], b
                    if last < 0:
                        last, last_b = last + PAIRS * UNITS, b - 1
                    act.wait_ge(pv_done, last_b.count(PAIRS * KB, last // 2 + 1 + START))
                    act.wait_ge(add_done, last_b.count(PAIRS * ADDS, adds_until(last) + START))
                for c in range(QC):
                    u = QC * unit + c
                    act.wait_ge(sc_ready, b.count(PAIRS * SCORES, u + 1 + START))
                    act.activation(P[:, BUFFER[unit], 512 * c:512 * c + 512], sc[BANK[u]][:, :],
                                   ACT.Exp).then_inc(exp_done, 1)

            def softmax_sum(b, t):
                act.wait_ge(nlmax_done, b.count(KB, t + 1 + START))
                act.activation(lexp[:, :], den[:, 0:E], ACT.Exp, bias=nlmax[:, :],
                               accum_out=lsum[:, :]).then_inc(lexp_done, 1)

            def copy_yT(b, t, bank):
                act.wait_ge(t1_ready, b.count(KB, t + 1 + START))
                act.wait_ge(h_ready, b.count(KB, t + START))
                act.activation(yT[:, :], bank[:, :], ACT.Copy).then_inc(yT_done, 1)

            def copy_hmT(b, t, bank):
                act.wait_ge(t2_ready, b.count(KB, t + 1 + START))
                act.wait_ge(z_ready, b.count(KB, t + START))
                act.activation(hmT[:, :], bank[:, :], ACT.Copy).then_inc(hmT_done, 1)

            def slot(b, p, tail, v_there, more):
                at = PLAN[tail, v_there]
                if more or p + 1 < PAIRS:
                    free_stacks(*after(b, p))
                for k in range(UNITS):
                    exp(b, p, k)
                    if k == 1 and not (v_there and p == 0):
                        copy_out(*before(b, p))
                    if k == DEN_AT and not (v_there and p == 0):
                        copy_denominators(*before(b, p))
                    kind, n = at.get((p, k), (None, None))
                    if kind == "max_t" and (more or p + 1 < PAIRS):
                        copy_max(*after(b, p), w)
                    elif kind == "qk" and (more or p < 6):
                        hi_part(b + (p == 6), QK_SLOTS[p], n, w)
                    elif kind == "v" and (more or p == 0):
                        copy_v(b + (p == 7), n, w)
                    elif kind == "t1":
                        copy_yT(b - 1, n, w)
                    elif kind == "h":
                        softmax_sum(b - 1, n)
                    elif kind == "t2":
                        copy_hmT(b - 1, n, w)

            for n in range(4):
                hi_part(first, 0, n, (w, pv)[n % 2])
            free_stacks(first, 0)
            for kb in range(KB):
                copy_v(first, kb, (w, pv)[kb % 2])
            copy_max(first, 0, w)
            for p in range(4):
                slot(first, p, False, True, True)
            with act.Fori(0, B - 1) as i:
                b = Batch(i)
                for p in range(4, 8):
                    slot(Batch(fresh(act, i)), p, True, False, True)
                for p in range(4):
                    slot(Batch(fresh(act, i), 1), p, True, False, True)
            for p in range(4, 8):
                slot(final, p, True, False, False)
            copy_out(final, PAIRS - 1)
            copy_denominators(final, PAIRS - 1)
            for kind, t in tail_pieces():
                if kind == "t1":
                    copy_yT(final, t, LAST_BANK[kind])
                elif kind == "h":
                    softmax_sum(final, t)
                elif kind == "t2":
                    copy_hmT(final, t, LAST_BANK[kind])

        @block.vector
        def _(dve):
            def lo_part(b, g, n, bank):
                hi, lo = ((Q_HI, Q_LO), (K_HI, K_LO))[n // 2]
                cols = slice(512 * (n % 2), 512 * (n % 2) + 512)
                dve.wait_ge(hi_done, b.count(4 * QUADS, 4 * g + n + 1 + START))
                dve.tensor_tensor(parts[:, lo, cols], bank[:, :], parts[:, hi, cols].bitcast(f32),
                                  ALU.subtract).then_inc(lo_done, 1)

            def max_item(b, q, m):
                at = MAXES * q + m
                dve.wait_ge(mx_ready, b.count(PAIRS * MAXES, at + 1 + START))
                dve.tensor_reduce(mxc[:, q % 2, m:m + 1], mx[MAX_BANK[at]][:, :], AX.X, ALU.max).then_inc(mx_done, 1)
                if m == MAXES - 1:
                    n = b.count(3 * PAIRS, 3 * q + START)
                    dve.wait_ge(mx_done, b.count(PAIRS * MAXES, at + 1 + START))
                    dve.tensor_reduce(mm[:, :], mxc[:, q % 2, :].rearrange("p (a c) -> p a c", c=QC), AX.X,
                                      ALU.max).then_inc(comb_done, 1)
                    if not (b.first and q == 0):
                        dve.wait_ge(mt_ready, b.count(PAIRS, q + START))
                    dve.wait_ge(comb_done, n + 1)
                    dve.tensor_scalar(nm[:, 0, :], mm[:, :], -1.0, None, ALU.mult).then_inc(comb_done, 1)
                    dve.wait_ge(comb_done, n + 2)
                    dve.scalar_tensor_tensor(out=nm[:, 1, :], in0=mm[:, :], scalar=-1.0, in1=nm[:, 0, :].bitcast(f32),
                                             op0=ALU.mult, op1=ALU.subtract).then_inc(comb_done, 1)

            def reciprocal_piece(b, p, n):
                dve.wait_ge(den_copied, b.count(PAIRS, p + 1 + START))
                dve.reciprocal(rden[:, 128 * n:128 * n + 128], rden[:, 128 * n:128 * n + 128]).then_inc(rden_done, 1)

            def normalise(b, p):
                dve.wait_ge(rden_done, b.count(PAIRS * 4, 4 * p + 4 + START))
                dve.wait_ge(pv_copied, b.count(PAIRS, p + 1 + START))
                if p == 0:
                    dve.wait_ge(o_ready, b.count(KB, START))
                for c in range(QC):
                    dve.tensor_tensor(attT[64 * (p % 2):64 * (p % 2) + 64, p // 2, 512 * c:512 * c + 512],
                                      pv_s[64 * c:64 * c + 64, :], rden[64 * c:64 * c + 64, :],
                                      ALU.mult).then_inc(norm_done, 1)

            def statistics(b, n, t):
                at = b.count(2 * KB, n * KB + t + 1 + START)
                dve.bn_stats(stats[:, t, :], r[:, t, :]).then_inc(stats_done, 1)
                if t % HALF == HALF - 1:
                    dve.wait_ge(stats_done, at)
                    dve.memset(settle[:, :], 0.0)
                    for tile in range(t - HALF + 1, t + 1):
                        done = dve.bn_aggr(mv[:, tile, :], stats[:, tile, :])
                    done.then_inc(mv_done, 1)

            def residual_attention(b, t, bank):
                if t == 0:
                    dve.wait_ge(r_loaded, b.count(16, 16))
                dve.wait_ge(o_ready, b.count(KB, t + 1 + START))
                dve.tensor_tensor(r[:, t, :], bank[:, :], r[:, t, :], ALU.add).then_inc(o_read, 1)
                dve.wait_ge(o_read, b.count(KB, t + 1 + START))
                statistics(b, 0, t)

            def residual_experts(b, t, bank):
                dve.wait_ge(z_ready, b.count(KB, t + 1 + START))
                dve.tensor_tensor(r[:, t, :], bank[:, :], r[:, t, :], ALU.add).then_inc(z_read, 1)
                dve.wait_ge(z_read, b.count(KB, t + 1 + START))
                statistics(b, 1, t)

            def layer_norm(b, n, half):
                dve.wait_ge(rstd_done, b.count(4, 2 * n + half + 1 + START))
                for t in range(HALF * half, HALF * half + HALF):
                    dve.tensor_scalar(r[:, t, :], r[:, t, :], mv[:, t, 0:1], rstd[:, t:t + 1], ALU.subtract,
                                      ALU.mult).then_inc((y_done, out_done)[n], 1)

            def gates(b, t, bank):
                at = b.count(KB * GATE_STEPS, t * GATE_STEPS + START)
                dve.wait_ge(h_ready, b.count(KB, t + 1 + START))
                dve.tensor_reduce(lmax[:, :], den[:, 0:E], AX.X, ALU.max).then_inc(gate_step, 1)
                dve.wait_ge(gate_step, at + 1)
                dve.tensor_scalar(nlmax[:, :], lmax[:, :], -1.0, None, ALU.mult).then_inc(nlmax_done, 1)
                dve.wait_ge(lexp_done, b.count(KB, t + 1 + START))
                dve.reciprocal(lrec[:, :], lsum[:, :]).then_inc(gate_step, 1)
                dve.scalar_tensor_tensor(out=eq[:, :], in0=den[:, 0:E], scalar=lmax[:, :], in1=rank[:, :],
                                         op0=ALU.is_ge, op1=ALU.mult).then_inc(gate_step, 1)
                dve.wait_ge(gate_step, at + 3)
                dve.tensor_reduce(eqm[:, :], eq[:, :], AX.X, ALU.max).then_inc(gate_step, 1)
                dve.wait_ge(gate_step, at + 4)
                dve.tensor_scalar(gate[:, :], eq[:, :], eqm[:, :], lrec[:, :], ALU.is_equal,
                                  ALU.mult).then_inc(gate_step, 1)
                dve.wait_ge(t2_ready, b.count(KB, t + START))
                dve.wait_ge(gate_step, at + 5)
                dve.scalar_tensor_tensor(out=hm[:, :].rearrange("p (e r) -> p e r", e=E),
                                         in0=bank[:, :].rearrange("p (e r) -> p e r", e=E), scalar=SCALING,
                                         in1=gate[:, :].unsqueeze(2).to_broadcast([128, E, R]),
                                         op0=ALU.mult, op1=ALU.mult).then_inc(hm_done, 1)

            def slot(b, p, tail, v_there, more):
                at = PLAN[tail, v_there]
                last = before(b, p)
                for k in range(UNITS):
                    if more or p + 1 < PAIRS:
                        for m in max_items(k):
                            max_item(*after(b, p), m)
                    if not (v_there and p == 0):
                        if REC_AT <= k < REC_AT + 4:
                            reciprocal_piece(*last, k - REC_AT)
                        if k == NORM_AT:
                            normalise(*last)
                    kind, n = at.get((p, k), (None, None))
                    if kind == "qk" and (more or p < 6):
                        lo_part(b + (p == 6), QK_SLOTS[p], n, w)
                    elif kind == "o":
                        residual_attention(b - 1, n, w)
                    elif kind == "h":
                        gates(b - 1, n, w)
                    elif kind == "z":
                        residual_experts(b - 1, n, w)
                    if tail and (p, k) in LN_APPLY:
                        layer_norm(b - 1, *LN_APPLY[p, k])

            start(dve, lo_done, mx_done, comb_done, rden_done, norm_done, o_read, stats_done, mv_done, y_done,
                  nlmax_done, gate_step, hm_done, z_read, out_done)
            dve.memset(stacks[3 * HD:KS, :, 0, :, :].bitcast(f32), 1.0).then_inc(const_ready, 1)
            dve.memset(ones[:, :], 1.0).then_inc(const_ready, 1)
            dve.memset(ones_row[:, :], 1.0).then_inc(const_ready, 1)
            for e in range(E):
                dve.memset(rank[:, e:e + 1], float(E - e)).then_inc(const_ready, 1)
            dve.wait_ge(const_ready, CONSTS)
            for n in range(4):
                lo_part(first, 0, n, (w, pv)[n % 2])
            for m in range(MAXES):
                max_item(first, 0, m)
            for p in range(4):
                slot(first, p, False, True, True)
            with dve.Fori(0, B - 1) as i:
                b = Batch(i)
                for p in range(4, 8):
                    slot(Batch(fresh(dve, i)), p, True, False, True)
                for p in range(4):
                    slot(Batch(fresh(dve, i), 1), p, True, False, True)
            for p in range(4, 8):
                slot(final, p, True, False, False)
            for n in range(4):
                reciprocal_piece(final, PAIRS - 1, n)
            normalise(final, PAIRS - 1)
            for t in range(KB):
                residual_attention(final, t, o_bank(t))
                if t % HALF == HALF - 1:
                    layer_norm(final, 0, t // HALF)
            for kind, t in tail_pieces():
                if kind == "h":
                    gates(final, t, LAST_BANK[kind])
                elif kind == "z":
                    residual_experts(final, t, LAST_BANK[kind])
                    if t % HALF == HALF - 1:
                        layer_norm(final, 1, t // HALF)


def kernel(L0_attn_x, L0_attn_wq, L0_attn_wk, L0_attn_wv, L0_attn_wo, L0_ffn_A, L0_ffn_B, L0_ffn_Wr, L0_ffn_br):
    import numpy as np
    import concourse.bacc as bacc
    from concourse.bass_utils import run_bass_kernel_spmd

    x = np.asarray(L0_attn_x)
    d = x.shape[-1]
    e, r = L0_ffn_A.shape[:2]
    arrays = {
        "xT": np.ascontiguousarray(x.reshape(-1, d).T),
        "x": np.ascontiguousarray(x),
        "wqT": np.ascontiguousarray(np.asarray(L0_attn_wq).T),
        "wkT": np.ascontiguousarray(np.asarray(L0_attn_wk).T),
        "wvT": np.ascontiguousarray(np.asarray(L0_attn_wv).T),
        "woT": np.ascontiguousarray(np.asarray(L0_attn_wo).T),
        "aT": np.ascontiguousarray(np.asarray(L0_ffn_A).reshape(e * r, d).T),
        "bT": np.ascontiguousarray(np.asarray(L0_ffn_B).transpose(0, 2, 1).reshape(e * r, d)),
        "wrT": np.ascontiguousarray(np.asarray(L0_ffn_Wr).T),
        "br": np.ascontiguousarray(np.asarray(L0_ffn_br).reshape(1, e)),
    }
    nc = bacc.Bacc("TRN2", target_bir_lowering=False, num_devices=1)
    args = [nc.dram_tensor(n, a.shape, mybir.dt.from_np(a.dtype), kind="ExternalInput").ap() for n, a in arrays.items()]
    out = nc.dram_tensor("out", x.shape, mybir.dt.float32, kind="ExternalOutput").ap()
    build_attention_lora_moe_block(nc, *args, out)
    result = run_bass_kernel_spmd(nc, [arrays], core_ids=[0])
    return result.results[0]["out"]
```

```python
from contextlib import ExitStack

import concourse.bass as bass
from concourse import mybir


class Batch:

    def __init__(self, loop, offset=0):
        self.loop, self.offset = loop, offset
        self.first = type(loop) is int and loop + offset == 0

    def __add__(self, n):
        return Batch(self.loop, self.offset + n)

    def __sub__(self, n):
        return Batch(self.loop, self.offset - n)

    def count(self, a_batch, n):
        return self.loop * a_batch + (self.offset * a_batch + n)


def build_attention_lora_moe_block(nc, xT, x, wqT, wkT, wvT, woT, aT, bT, wrT, br, out):
    f32, f32r = mybir.dt.float32, mybir.dt.float32r
    ALU, ACT, AX = mybir.AluOpType, mybir.ActivationFunctionType, mybir.AxisListType

    B, S, D = x.shape
    E = br.shape[1]
    R = aT.shape[1] // E
    HD = 32
    H = D // HD
    KT = D // 128
    QC = S // 512
    KB = S // 128
    PAIRS = H // 2
    QUADS = H // 4
    UNITS = 2 * KB
    SCORES = UNITS * QC
    MAXES = 2 * KB * QC
    ADDS = UNITS - 4
    KS = 3 * HD + 2
    NP, NSC, NMX = 6, 2, 3
    HALF = KB // 2
    START = 1
    EPS, SCALING = 1e-5, 1.0 / R
    STACK_INCS = 6 * 16
    K_HI, K_LO, Q_HI, Q_LO = range(4)

    first, final = Batch(0), Batch(B - 1)
    ctx = ExitStack()
    with ctx:
        def sb(name, shape, dt=f32):
            return ctx.enter_context(nc.sbuf_tensor(name, shape, dt))

        def ps(name, shape):
            return ctx.enter_context(nc.psum_tensor(name, shape, f32))

        def sem(name):
            return ctx.enter_context(nc.semaphore(name))

        wq_s, wk_s, wv_s, wo_s = (sb(n, [128, KT, D]) for n in ("wq_s", "wk_s", "wv_s", "wo_s"))
        a_s, b_s = sb("a_s", [128, KT, E * R]), sb("b_s", [128, KT, D])
        wr_s, br_s = sb("wr_s", [128, KT, E]), sb("br_s", [1, E])
        xT_s = sb("xT_s", [128, KT, S])
        parts = sb("parts", [128, 4, S], f32r)
        stacks = sb("stacks", [128, 2, 2, 2, S], f32r)
        V = sb("V", [128, KB, D])
        P = sb("P", [128, NP, S])
        Psum = sb("Psum", [128, 2, S])
        attT = sb("attT", [128, KT, S])
        pv_s, rden = sb("pv_s", [128, 512]), sb("rden", [128, 512])
        r = sb("r", [128, KB, D])
        yT, hm, hmT = sb("yT", [128, D]), sb("hm", [128, E * R]), sb("hmT", [128, E * R])
        mxc = sb("mxc", [128, 2, MAXES])
        mm = sb("mm", [128, 2 * KB])
        nm = sb("nm", [128, 2, 2 * KB], f32r)
        mrow = sb("mrow", [32, 128], f32r)
        ident, ones, ones_row = sb("ident", [128, 128]), sb("ones", [128, 32]), sb("ones_row", [1, 128])
        rank = sb("rank", [128, E])
        mhalf, eps_s, settle = sb("mhalf", [128, HALF]), sb("eps_s", [128, HALF]), sb("settle", [128, 1])
        stats, mv = sb("stats", [128, KB, 6]), sb("mv", [128, KB, 2])
        ve, rstd = sb("ve", [128, HALF]), sb("rstd", [128, KB])
        lmax, nlmax = sb("lmax", [128, 1]), sb("nlmax", [128, 1])
        lexp, lsum, lrec = sb("lexp", [128, E]), sb("lsum", [128, 1]), sb("lrec", [128, 1])
        eq, eqm, gate = sb("eq", [128, E]), sb("eqm", [128, 1]), sb("gate", [128, E])

        sc = [ps(f"sc{i}", [128, 512]) for i in range(NSC)]
        mx = [ps(f"mx{i}", [128, 512]) for i in range(NMX)]
        pv, den, w = ps("pv", [128, 512]), ps("den", [128, 512]), ps("w", [128, 512])

        const_ready, ident_zero, x_loaded = sem("const_ready"), sem("ident_zero"), sem("x_loaded")
        w_loaded = {n: sem(f"{n}_loaded") for n in ("wq", "wk", "wv", "tail_w")}
        qk_ready, hi_done, lo_done = sem("qk_ready"), sem("hi_done"), sem("lo_done")
        v_ready, v_done = sem("v_ready"), sem("v_done")
        stack_free, stack_loaded = sem("stack_free"), [sem(f"stack_loaded{i}") for i in range(2)]
        m_loaded = sem("m_loaded")
        mx_ready, mx_done, comb_done = sem("mx_ready"), sem("mx_done"), sem("comb_done")
        mt_ready, mrow_done = sem("mt_ready"), sem("mrow_done")
        sc_ready, exp_done, pv_done, pv_copied = sem("sc_ready"), sem("exp_done"), sem("pv_done"), sem("pv_copied")
        first_added, add_done, den_done, den_copied = sem("first_added"), sem("add_done"), sem("den_done"), sem("den_copied")
        rden_done, norm_done = sem("rden_done"), sem("norm_done")
        part_ready, part_read = sem("part_ready"), sem("part_read")
        r_loaded, o_ready, o_read = sem("r_loaded"), sem("o_ready"), sem("o_read")
        stats_done, mv_done, ve_done, rstd_done = sem("stats_done"), sem("mv_done"), sem("ve_done"), sem("rstd_done")
        y_done, t1_ready, yT_done = sem("y_done"), sem("t1_ready"), sem("yT_done")
        h_ready, h_copied = sem("h_ready"), sem("h_copied")
        nlmax_done, lexp_done, gate_step, hm_done = sem("nlmax_done"), sem("lexp_done"), sem("gate_step"), sem("hm_done")
        t2_ready, hmT_done, z_ready, z_read = sem("t2_ready"), sem("hmT_done"), sem("z_ready"), sem("z_read")
        out_done, out_stored = sem("out_done"), [sem(f"out_stored{i}") for i in range(2)]

        MAX_FIRST, MAX_LAST, MAX_T = 3, 12, 13
        ADD_AT = (3, 4)
        DEN_AT, REC_AT = 3, (14, 15)
        SPLIT = 6
        LAST_Z = 10
        LONG = ("qk", "v", "o", "h", "z")
        V_EARLY = 6
        QK_SLOTS = {0: 1, 2: 2, 4: 3, 6: 0}

        def tail_pieces():
            pieces = [("t1", 0)]
            for t in range(KB):
                pieces += [("h", t)] + [("t1", t + 1)] * (t + 1 < KB) + [("z", t - 1)] * (t > 0) + [("t2", t)]
            return pieces + [("z", KB - 1)]

        def last_tail():
            pieces = [("o", t) for t in range(HALF)]
            for piece in tail_pieces():
                pieces.append(piece)
                if piece[0] == "h" and piece[1] < 2:
                    pieces += [("o", HALF + 2 * piece[1] + n) for n in range(2)]
            return pieces

        def plan(tail, last):
            at = {(p, MAX_T): ("max_t", None) for p in range(PAIRS)}
            if last:
                for t, k in enumerate((6, 7, 8, 9, 10, 11, 12, 14)):
                    at[7, k] = ("o_part", t)
                return at
            for p, steps in ((0, (4, 5, 6, 7)), (2, (4, 7, 10, 12)), (4, (4, 7, 10, 12)), (6, (7, 9, 11, 14))):
                for n, k in enumerate(steps):
                    at[p, k] = ("qk", n)
            for kb, k in enumerate((4, 6, 8, 10, 12, 15)):
                at[7, k] = ("v", kb)
            at[0, 0], at[0, 2] = ("v", V_EARLY), ("v", V_EARLY + 1)
            if tail:
                for t, k in enumerate((1, 2, 4, 6, 8, 10, 14, 15)):
                    at[1, k] = ("o", t)
                pieces = tail_pieces()
                weight = {"t1": 2, "h": 5, "z": 4, "t2": 2}
                total = sum(weight[kind] for kind, _ in pieces)
                spots = [(p, k) for p in range(2, SPLIT) for k in range(UNITS)
                         if (p, k) <= (SPLIT - 1, LAST_Z) and (p, k) not in at]
                placed, spent = 0, 0
                for n, spot in enumerate(spots):
                    if placed < len(pieces) and spent * (len(spots) - 1) <= total * n \
                            and not (pieces[placed][0] == "h" and spot[1] in (DEN_AT - 1, DEN_AT)):
                        at[spot] = pieces[placed]
                        spent += weight[pieces[placed][0]]
                        placed += 1
                assert placed == len(pieces)
            return at

        def position(spot):
            return UNITS * spot[0] + spot[1]

        PLAN = {flags: plan(*flags) for flags in ((False, False), (True, False), (True, True))}
        GATES_AT = {divmod(position(spot) + 1, UNITS): t for spot, (kind, t) in PLAN[True, False].items() if kind == "h"}
        LN_STATS, LN_APPLY = {}, {}
        for spot, (kind, t) in PLAN[True, False].items():
            if kind in ("o", "z") and t % HALF == HALF - 1:
                n = int(kind == "z")
                LN_STATS[spot] = (n, t // HALF)
                for tile in range(HALF):
                    LN_APPLY[divmod(position(spot) + 2 + tile, UNITS)] = (n, t - HALF + 1 + tile)

        def after(b, p):
            return (b, p + 1) if p + 1 < PAIRS else (b + 1, 0)

        def before(b, p):
            return (b, p - 1) if p else (b - 1, PAIRS - 1)

        def max_items(at, p, k):
            long = [at.get((p, step), ("", 0))[0] in LONG for step in range(MAX_LAST + 1)]
            begin = MAX_FIRST if any(long[:MAX_FIRST]) else MAX_FIRST + 1
            time = [5 if is_long else 2 for is_long in long[begin:]]
            if not begin <= k <= MAX_LAST:
                return range(0)
            until = [round(MAXES * sum(time[:n]) / sum(time)) for n in (k - begin, k - begin + 1)]
            return range(*until)

        def stacks_there(b, q):
            return stack_loaded[q % 2], b.count(PAIRS // 2 * STACK_INCS, (q // 2 + 1) * STACK_INCS)

        def adds_until(unit):
            p, k = divmod(unit, UNITS)
            return ADDS * p + k - 3

        CONSTS = 3 + 3 + E
        GATE_STEPS = 4 + 1
        LAST_BANK = {"t1": mx[0], "h": mx[2], "t2": mx[1], "z": sc[1]}

        def o_bank(t):
            return (w, sc[0])[t % 2]

        def rotate(count, buffers, shifted):
            at = [n % buffers for n in range(count)]
            at[count - len(shifted):] = shifted
            twice = at + at
            return at, [max(m for m in range(count + n) if twice[m] == at[n]) - count for n in range(count)]

        BUFFER, BUFFER_BEFORE = rotate(PAIRS * UNITS, NP, [2, 3])
        BANK, BANK_BEFORE = rotate(PAIRS * SCORES, NSC, [])
        MAX_BANK, MAX_BANK_BEFORE = rotate(PAIRS * MAXES, NMX, [1])


        def fresh(engine, loop):
            copy = engine.alloc_register()
            engine.reg_mov(copy, loop)
            return engine.snap(copy, donate=True)

        def start(engine, *semaphores):
            for s in semaphores:
                engine.sem_inc(s, START)

        block = ctx.enter_context(nc.Block())

        @block.sync
        def _(sp):
            xT_v = xT.rearrange("(k p) t -> p k t", p=128)

            def load_stacks(b, q):
                sp.wait_ge(stack_free, b.count(PAIRS, q + 1 + START))
                for n, (k_part, q_part) in enumerate(((K_HI, Q_HI), (K_LO, Q_HI), (K_HI, Q_LO))):
                    for i in range(2):
                        row = 2 * HD * (q % 2) + HD * i
                        sp.dma_start(stacks[HD * n:HD * n + HD, q % 2, :, i, :].bitcast(f32),
                                     parts[row:row + HD, k_part:q_part + 1:q_part - k_part, :].bitcast(f32)) \
                            .then_inc(stack_loaded[q % 2], 16)

            def load_max(b, q):
                sp.wait_ge(mrow_done, b.count(PAIRS, q + 1 + START))
                for n in range(2):
                    sp.dma_start(stacks[3 * HD + n:3 * HD + n + 1, q % 2, 1, :, :].bitcast(f32)
                                 .rearrange("a i (r t) -> a (i r) t", t=128),
                                 mrow[16 * n:16 * n + 16, :].bitcast(f32)).then_inc(m_loaded, 16)

            def rows(tensor, b, t, n):
                return tensor.rearrange("b s d -> (b s) d")[bass.ds(b.count(S, 128 * t), 128 * n), :] \
                    .rearrange("(t p) d -> p t d", p=128)

            def store(b, half):
                sp.wait_ge(out_done, b.count(KB, HALF * (half + 1) + START))
                sp.dma_start(rows(out, b, HALF * half, HALF), r[:, HALF * half:HALF * half + HALF, :]) \
                    .then_inc(out_stored[half], 16)

            def slot(b, p, tail, more):
                if more or p + 1 < PAIRS:
                    load_stacks(*after(b, p))
                if p == SPLIT and more:
                    sp.wait_ge(qk_ready, b.count(4 * QUADS, 4 * QUADS + START))
                    sp.dma_start(xT_s[:, :, :], xT_v[:, :, bass.ds(b.count(S, S), S)]).then_inc(x_loaded, 16)
                if p == 7:
                    for stored in out_stored:
                        sp.wait_ge(stored, b.count(16, 16))
                    sp.dma_start(r[:, :, :], rows(x, b, 0, KB)).then_inc(r_loaded, 16)
                if more or p + 1 < PAIRS:
                    load_max(*after(b, p))
                if p in (SPLIT - 2, SPLIT - 1) and tail:
                    store(b - 1, p - (SPLIT - 2))

            for stored in out_stored:
                sp.sem_inc(stored, 16)
            sp.dma_start(xT_s[:, :, :], xT_v[:, :, 0:S]).then_inc(x_loaded, 16)
            load_stacks(first, 0)
            load_max(first, 0)
            for p in range(SPLIT):
                slot(first, p, False, True)
            with sp.Fori(0, B - 1) as i:
                b = Batch(i)
                for p in range(SPLIT, PAIRS):
                    slot(Batch(fresh(sp, i)), p, True, True)
                for p in range(SPLIT):
                    slot(Batch(fresh(sp, i), 1), p, True, True)
            for p in range(SPLIT, PAIRS):
                slot(final, p, True, False)
            store(final, 0)
            store(final, 1)
            for stored in out_stored:
                sp.wait_ge(stored, B * 16 + 16)

        @block.gpsimd
        def _(pool):
            start(pool, add_done, ve_done, rstd_done)
            pool.dma_start(wk_s[:, :, :], wkT.rearrange("(k p) n -> p k n", p=128)).then_inc(w_loaded["wk"], 16)
            pool.dma_start(wv_s[:, :, :], wvT.rearrange("(k p) n -> p k n", p=128)).then_inc(w_loaded["wv"], 16)
            for s, d in ((wo_s, woT), (a_s, aT), (b_s, bT), (wr_s, wrT)):
                pool.dma_start(s[:, :, :], d.rearrange("(k p) n -> p k n", p=128)).then_inc(w_loaded["tail_w"], 16)
            pool.dma_start(br_s[:, :], br).then_inc(w_loaded["tail_w"], 16)
            pool.memset(ident[:, :], 0.0).then_inc(ident_zero, 1)
            pool.wait_ge(ident_zero, 1)
            pool.affine_select(out=ident[:, :], in_=ident[:, :], compare_op=ALU.not_equal, fill=1.0,
                               base=0, pattern=[[-1, 128]], channel_multiplier=1).then_inc(const_ready, 1)
            pool.memset(mhalf[:, :], -0.5).then_inc(const_ready, 1)
            pool.memset(eps_s[:, :], EPS).then_inc(const_ready, 1)
            pool.wait_ge(const_ready, CONSTS)

            def add(b, p, k):
                unit = UNITS * p + k
                pool.wait_ge(exp_done, b.count(PAIRS * SCORES, QC * (unit + 1) + START))
                if k < 6:
                    pool.wait_ge(first_added, b.count(PAIRS * 2, 2 * p + k - 3 + START))
                else:
                    pool.wait_ge(add_done, b.count(PAIRS * ADDS, ADDS * p + k - 5 + START))
                pool.tensor_tensor(Psum[:, k % 2, :], Psum[:, k % 2, :], P[:, BUFFER[unit], :],
                                   ALU.add).then_inc(add_done, 1)

            def reciprocal_deviation(b, n, half):
                at = b.count(4, 2 * n + half + 1 + START)
                tiles = slice(HALF * half, HALF * half + HALF)
                pool.wait_ge(mv_done, at)
                pool.tensor_tensor(ve[:, :], mv[:, tiles, 1], eps_s[:, :], ALU.add).then_inc(ve_done, 1)
                pool.wait_ge(ve_done, at)
                pool.tensor_tensor(rstd[:, tiles], ve[:, :], mhalf[:, :], ALU.pow).then_inc(rstd_done, 1)

            def slot(b, p, tail):
                for k in range(UNITS):
                    if k >= 4:
                        add(b, p, k)
                    if tail and (p, k) in LN_STATS:
                        reciprocal_deviation(b - 1, *LN_STATS[p, k])

            for p in range(SPLIT):
                slot(first, p, False)
            with pool.Fori(0, B - 1) as i:
                b = Batch(i)
                for p in range(SPLIT, PAIRS):
                    slot(Batch(fresh(pool, i)), p, True)
                for p in range(SPLIT):
                    slot(Batch(fresh(pool, i), 1), p, True)
            for p in range(SPLIT, PAIRS):
                slot(final, p, True)
            for n in range(2):
                for half in range(2):
                    reciprocal_deviation(final, n, half)

        @block.tensor
        def _(pe):
            reader = {}

            def take(bank, semaphore, value):
                if bank.name in reader:
                    pe.wait_ge(*reader[bank.name])
                reader[bank.name] = (semaphore, value + START)

            def qk(b, g, n, bank, between=None):
                ws, c = (wq_s, wk_s)[n // 2], n % 2
                if n == 0:
                    pe.wait_ge(x_loaded, b.count(16, 16))
                take(bank, lo_done, b.count(4 * QUADS, 4 * g + n + 1))
                for kt in range(KT):
                    done = pe.matmul(bank[:, :], ws[:, kt, 128 * g:128 * g + 128], xT_s[:, kt, 512 * c:512 * c + 512],
                                     start=(kt == 0), stop=(kt == KT - 1))
                    if between and kt < KT - 1:
                        between()
                done.then_inc(qk_ready, 1)

            def v(b, kb, bank, between=None):
                take(bank, v_done, b.count(KB, kb + 1))
                for kt in range(KT):
                    done = pe.matmul(bank[:, :], xT_s[:, kt, 128 * kb:128 * kb + 128], wv_s[:, kt, :],
                                     start=(kt == 0), stop=(kt == KT - 1))
                    if between and kt < KT - 1:
                        between()
                done.then_inc(v_ready, 1)

            def max_item(b, q, m):
                i, qb, c = m // (KB * QC), m // QC % KB, m % QC
                at = MAXES * q + m
                if m == 0:
                    pe.wait_ge(*stacks_there(b, q))
                if not (b.first and at < NMX):
                    pe.wait_ge(mx_done, b.count(PAIRS * MAXES, MAX_BANK_BEFORE[at] + 1 + START))
                pe.matmul(mx[MAX_BANK[at]][:, :], stacks[0:3 * HD, q % 2, 1, i, 128 * qb:128 * qb + 128],
                          stacks[0:3 * HD, q % 2, 0, i, 512 * c:512 * c + 512], start=True, stop=True).then_inc(mx_ready, 1)

            def max_t(b, q, bank):
                pe.wait_ge(comb_done, b.count(3 * PAIRS, 3 * q + 3 + START))
                take(bank, mrow_done, b.count(PAIRS, q + 1))
                pe.transpose(bank[0:32, 0:128], nm[:, :, :].rearrange("p a c -> p (a c)").bitcast(f32),
                             ident[:, :]).then_inc(mt_ready, 1)

            def score(b, p, k, c):
                kb, i = k // 2, k % 2
                u = SCORES * p + QC * k + c
                if k == 0 and c == 0:
                    pe.wait_ge(*stacks_there(b, p))
                    pe.wait_ge(m_loaded, b.count(PAIRS * 32, 32 * p + 32))
                if not (b.first and u < NSC):
                    pe.wait_ge(exp_done, b.count(PAIRS * SCORES, BANK_BEFORE[u] + 1 + START))
                pe.matmul(sc[BANK[u]][:, :], stacks[0:KS, p % 2, 0, i, 128 * kb:128 * kb + 128],
                          stacks[0:KS, p % 2, 1, i, 512 * c:512 * c + 512], start=True, stop=True).then_inc(sc_ready, 1)

            def out_block(b, p, kb):
                pe.wait_ge(exp_done, b.count(PAIRS * SCORES, QC * (UNITS * p + 2 * kb + 2) + START))
                if p == 0:
                    pe.wait_ge(v_done, b.count(KB, kb + 1 + START))
                if kb == 0 and not (b.first and p == 0):
                    pe.wait_ge(pv_copied, b.count(PAIRS, p + START))
                for c in range(QC):
                    for i in range(2):
                        at = HD * (2 * c + i)
                        h = 2 * p + i
                        done = pe.matmul(pv[at:at + HD, :], V[:, kb, HD * h:HD * h + HD],
                                         P[:, BUFFER[UNITS * p + 2 * kb + i], 512 * c:512 * c + 512],
                                         start=(kb == 0), stop=(kb == KB - 1))
                done.then_inc(pv_done, 1)

            def denominators(b, p):
                pe.wait_ge(add_done, b.count(PAIRS * ADDS, ADDS * (p + 1) + START))
                if not (b.first and p == 0):
                    pe.wait_ge(den_copied, b.count(PAIRS, p + START))
                take(den, den_copied, b.count(PAIRS, p + 1))
                for c in range(QC):
                    for i in range(2):
                        at = HD * (2 * c + i)
                        done = pe.matmul(den[at:at + HD, :], ones[:, :], Psum[:, i, 512 * c:512 * c + 512],
                                         start=True, stop=True)
                done.then_inc(den_done, 1)

            def o_part(t, bank, between):
                if t == 0:
                    pe.wait_ge(norm_done, final.count(2 * PAIRS, 2 * PAIRS - 4 + START))
                take(bank, part_read, t + 1)
                for kt in range(KT - 1):
                    done = pe.matmul(bank[:, :], attT[:, kt, 128 * t:128 * t + 128], wo_s[:, kt, :],
                                     start=(kt == 0), stop=(kt == KT - 2))
                    between()
                done.then_inc(part_ready, 1)

            def o(b, t, bank, between=None, chunks=range(KT)):
                if t == 0:
                    pe.wait_ge(norm_done, b.count(2 * PAIRS, 2 * PAIRS + START))
                take(bank, o_read, b.count(KB, t + 1))
                for kt in chunks:
                    done = pe.matmul(bank[:, :], attT[:, kt, 128 * t:128 * t + 128], wo_s[:, kt, :],
                                     start=(kt == chunks[0]), stop=(kt == KT - 1))
                    if between and kt < KT - 1:
                        between()
                done.then_inc(o_ready, 1)

            def t1(b, t, bank, between=None):
                take(bank, yT_done, b.count(KB, t + 1))
                pe.wait_ge(y_done, b.count(KB, t + 1 + START))
                for kt in range(KT):
                    done = pe.transpose(bank[:, 128 * kt:128 * kt + 128], r[:, t, 128 * kt:128 * kt + 128], ident[:, :])
                done.then_inc(t1_ready, 1)

            def h(b, t, bank, between=None):
                pe.wait_ge(yT_done, b.count(KB, t + 1 + START))
                take(den, hm_done, b.count(KB, t + 1))
                take(bank, h_copied, b.count(KB, t + 1))
                for kt in range(KT):
                    pe.matmul(den[:, 0:E], yT[:, 128 * kt:128 * kt + 128], wr_s[:, kt, :], start=(kt == 0), stop=False)
                pe.matmul(den[:, 0:E], ones_row[:, :], br_s[:, :], start=False, stop=True)
                for kt in range(KT):
                    done = pe.matmul(bank[:, :], yT[:, 128 * kt:128 * kt + 128], a_s[:, kt, :],
                                     start=(kt == 0), stop=(kt == KT - 1))
                    if between and kt < KT - 1:
                        between()
                done.then_inc(h_ready, 1)

            def t2(b, t, bank, between=None):
                take(bank, hmT_done, b.count(KB, t + 1))
                pe.wait_ge(hm_done, b.count(KB, t + 1 + START))
                for kt in range(KT):
                    done = pe.transpose(bank[:, 128 * kt:128 * kt + 128], hm[:, 128 * kt:128 * kt + 128], ident[:, :])
                done.then_inc(t2_ready, 1)

            def z(b, t, bank, between=None):
                pe.wait_ge(hmT_done, b.count(KB, t + 1 + START))
                take(bank, z_read, b.count(KB, t + 1))
                for kt in range(KT):
                    done = pe.matmul(bank[:, :], hmT[:, 128 * kt:128 * kt + 128], b_s[:, kt, :],
                                     start=(kt == 0), stop=(kt == KT - 1))
                    if between and kt < KT - 1:
                        between()
                done.then_inc(z_ready, 1)

            def slot(b, p, tail, opening, more):
                at = PLAN[tail, not more]
                for k in range(UNITS):
                    maxima = iter(max_items(at, p, k) if more or p + 1 < PAIRS else ())

                    def between():
                        for m in maxima:
                            max_item(*after(b, p), m)
                            return

                    kind, n = at.get((p, k), (None, None))
                    score(b, p, k, 0)
                    between()
                    if kind not in LONG:
                        score(b, p, k, 1)
                        between()
                    if k == 1 and not (opening and p == 0):
                        out_block(*before(b, p), KB - 1)
                    if k % 2 == 1 and k >= 3:
                        out_block(b, p, (k - 3) // 2)
                    if kind in LONG:
                        score(b, p, k, 1)
                        between()
                    if k == DEN_AT and not (opening and p == 0):
                        denominators(*before(b, p))
                    if kind in ("t1", "t2"):
                        for m in maxima:
                            max_item(*after(b, p), m)
                    if kind == "max_t" and (more or p + 1 < PAIRS):
                        max_t(*after(b, p), w)
                    elif kind == "qk" and (more or p < 6):
                        qk(b + (p == 6), QK_SLOTS[p], n, w, between)
                    elif kind == "v" and (more or p == 0):
                        v(b + (p == 7), n, w, between)
                    elif kind == "o_part":
                        o_part(n, w, between)
                    elif kind in ("o", "t1", "h", "t2", "z"):
                        {"o": o, "t1": t1, "h": h, "t2": t2, "z": z}[kind](b - 1, n, w, between)
                    for m in maxima:
                        max_item(*after(b, p), m)

            start(pe, part_ready, qk_ready, v_ready, mx_ready, mt_ready, sc_ready, pv_done, den_done, o_ready, t1_ready, h_ready,
                  t2_ready, z_ready)
            pe.wait_ge(const_ready, CONSTS)
            pe.wait_ge(w_loaded["wq"], 16)
            pe.wait_ge(w_loaded["wk"], 16)
            for n in range(4):
                qk(first, 0, n, (w, pv)[n % 2])
            pe.wait_ge(w_loaded["wv"], 16)
            maxima = iter(range(MAXES))

            def few_maxima():
                for _, m in zip(range(NMX), maxima):
                    max_item(first, 0, m)

            for kb in range(V_EARLY):
                v(first, kb, (w, pv)[kb % 2], few_maxima if kb >= 2 else None)
                if kb >= 2:
                    few_maxima()
            assert not list(maxima)
            max_t(first, 0, w)
            pe.wait_ge(v_done, V_EARLY + START)
            for p in range(SPLIT):
                slot(first, p, False, True, True)
            pe.wait_ge(w_loaded["tail_w"], 16 * 5)
            with pe.Fori(0, B - 1) as i:
                b = Batch(i)
                reader[w.name] = (mrow_done, b.count(PAIRS, SPLIT + 1 + START))
                reader[den.name] = (hm_done, b.count(KB, START))
                for p in range(SPLIT, PAIRS):
                    slot(Batch(fresh(pe, i)), p, True, False, True)
                for p in range(SPLIT):
                    slot(Batch(fresh(pe, i), 1), p, True, False, True)
            reader[w.name] = (mrow_done, final.count(PAIRS, SPLIT + 1 + START))
            reader[den.name] = (hm_done, final.count(KB, START))
            for p in range(SPLIT, PAIRS):
                slot(final, p, True, False, False)
            out_block(final, PAIRS - 1, KB - 1)
            denominators(final, PAIRS - 1)
            pe.wait_ge(exp_done, B * PAIRS * SCORES + START)
            pe.wait_ge(mx_done, B * PAIRS * MAXES + START)
            for kind, t in last_tail():
                if kind == "o":
                    o(final, t, o_bank(t), chunks=range(KT - 1, KT))
                else:
                    {"t1": t1, "h": h, "t2": t2, "z": z}[kind](final, t, LAST_BANK[kind])

        @block.scalar
        def _(act):
            start(act, h_copied, hi_done, v_done, mrow_done, exp_done, pv_copied, den_copied, yT_done, lexp_done, hmT_done, stack_free)
            act.dma_start(wq_s[:, :, :], wqT.rearrange("(k p) n -> p k n", p=128)).then_inc(w_loaded["wq"], 16)

            def hi_part(b, g, n, bank):
                act.wait_ge(qk_ready, b.count(4 * QUADS, 4 * g + n + 1 + START))
                if n == 0 and not (b.first and g == 0):
                    for back in (1, 2):
                        act.wait_ge(*(stacks_there(b, 2 * g - back) if g else stacks_there(b - 1, PAIRS - back)))
                act.activation(parts[:, (Q_HI, K_HI)[n // 2], 512 * (n % 2):512 * (n % 2) + 512], bank[:, :],
                               ACT.Copy).then_inc(hi_done, 1)

            def copy_v(b, kb, bank):
                act.wait_ge(v_ready, b.count(KB, kb + 1 + START))
                if not (b.first):
                    act.wait_ge(pv_done, b.count(PAIRS * KB, -KB + kb + 1 + START))
                act.activation(V[:, kb, :], bank[:, :], ACT.Copy).then_inc(v_done, 1)

            def copy_max(b, q, bank):
                act.wait_ge(mt_ready, b.count(PAIRS, q + 1 + START))
                if not (b.first and q == 0):
                    act.wait_ge(m_loaded, b.count(PAIRS * 32, 32 * q))
                act.activation(mrow[:, :], bank[0:32, 0:128], ACT.Copy).then_inc(mrow_done, 1)

            def copy_out(b, p):
                act.wait_ge(pv_done, b.count(PAIRS * KB, KB * p + KB + START))
                act.wait_ge(norm_done, b.count(PAIRS * 2, 2 * p + START))
                act.activation(pv_s[:, :], pv[:, :], ACT.Copy).then_inc(pv_copied, 1)

            def copy_denominators(b, p):
                act.wait_ge(den_done, b.count(PAIRS, p + 1 + START))
                act.wait_ge(norm_done, b.count(PAIRS * 2, 2 * p + START))
                act.activation(rden[:, :], den[:, :], ACT.Copy).then_inc(den_copied, 1)

            def free_stacks(b, q):
                act.wait_ge(lo_done, b.count(4 * QUADS, 4 * (q // 2) + 4 + START))
                act.sem_inc(stack_free, 1)

            def exp(b, p, k):
                unit = UNITS * p + k
                if not (b.first and unit < NP):
                    last, last_b = BUFFER_BEFORE[unit], b
                    if last < 0:
                        last, last_b = last + PAIRS * UNITS, b - 1
                    act.wait_ge(pv_done, last_b.count(PAIRS * KB, last // 2 + 1 + START))
                    if last % UNITS < 4:
                        act.wait_ge(first_added, last_b.count(PAIRS * 2, last // UNITS * 2 + last % 2 + 1 + START))
                    else:
                        act.wait_ge(add_done, last_b.count(PAIRS * ADDS, adds_until(last) + START))
                for c in range(QC):
                    u = QC * unit + c
                    act.wait_ge(sc_ready, b.count(PAIRS * SCORES, u + 1 + START))
                    act.activation(P[:, BUFFER[unit], 512 * c:512 * c + 512], sc[BANK[u]][:, :],
                                   ACT.Exp).then_inc(exp_done, 1)

            def copy_h(b, t, bank):
                act.wait_ge(h_ready, b.count(KB, t + 1 + START))
                act.wait_ge(t2_ready, b.count(KB, t + START))
                act.activation(hm[:, :], bank[:, :], ACT.Copy).then_inc(h_copied, 1)

            def softmax_sum(b, t):
                act.wait_ge(nlmax_done, b.count(KB, t + 1 + START))
                act.activation(lexp[:, :], den[:, 0:E], ACT.Exp, bias=nlmax[:, :],
                               accum_out=lsum[:, :]).then_inc(lexp_done, 1)

            def copy_yT(b, t, bank):
                act.wait_ge(t1_ready, b.count(KB, t + 1 + START))
                act.wait_ge(h_ready, b.count(KB, t + START))
                act.activation(yT[:, :], bank[:, :], ACT.Copy).then_inc(yT_done, 1)

            def copy_hmT(b, t, bank):
                act.wait_ge(t2_ready, b.count(KB, t + 1 + START))
                act.wait_ge(z_ready, b.count(KB, t + START))
                act.activation(hmT[:, :], bank[:, :], ACT.Copy).then_inc(hmT_done, 1)

            def slot(b, p, tail, opening, more):
                at = PLAN[tail, not more]
                if more or p + 1 < PAIRS:
                    free_stacks(*after(b, p))
                for k in range(UNITS):
                    exp(b, p, k)
                    if k == 1 and not (opening and p == 0):
                        copy_out(*before(b, p))
                    if k == DEN_AT and not (opening and p == 0):
                        copy_denominators(*before(b, p))
                    if tail and (p, k) in GATES_AT:
                        softmax_sum(b - 1, GATES_AT[p, k])
                    kind, n = at.get((p, k), (None, None))
                    if kind == "max_t" and (more or p + 1 < PAIRS):
                        copy_max(*after(b, p), w)
                    elif kind == "qk" and (more or p < 6):
                        hi_part(b + (p == 6), QK_SLOTS[p], n, w)
                    elif kind == "v" and (more or p == 0):
                        copy_v(b + (p == 7), n, w)
                    elif kind == "t1":
                        copy_yT(b - 1, n, w)
                    elif kind == "h":
                        copy_h(b - 1, n, w)
                    elif kind == "t2":
                        copy_hmT(b - 1, n, w)

            for n in range(4):
                hi_part(first, 0, n, (w, pv)[n % 2])
            free_stacks(first, 0)
            for kb in range(V_EARLY):
                copy_v(first, kb, (w, pv)[kb % 2])
            copy_max(first, 0, w)
            for p in range(SPLIT):
                slot(first, p, False, True, True)
            with act.Fori(0, B - 1) as i:
                b = Batch(i)
                for p in range(SPLIT, PAIRS):
                    slot(Batch(fresh(act, i)), p, True, False, True)
                for p in range(SPLIT):
                    slot(Batch(fresh(act, i), 1), p, True, False, True)
            for p in range(SPLIT, PAIRS):
                slot(final, p, True, False, False)
            copy_out(final, PAIRS - 1)
            copy_denominators(final, PAIRS - 1)
            for kind, t in last_tail():
                if kind == "t1":
                    copy_yT(final, t, LAST_BANK[kind])
                elif kind == "h":
                    copy_h(final, t, LAST_BANK[kind])
                    softmax_sum(final, t)
                elif kind == "t2":
                    copy_hmT(final, t, LAST_BANK[kind])

        @block.vector
        def _(dve):
            def lo_part(b, g, n, bank):
                hi, lo = ((Q_HI, Q_LO), (K_HI, K_LO))[n // 2]
                cols = slice(512 * (n % 2), 512 * (n % 2) + 512)
                dve.wait_ge(hi_done, b.count(4 * QUADS, 4 * g + n + 1 + START))
                dve.tensor_tensor(parts[:, lo, cols], bank[:, :], parts[:, hi, cols].bitcast(f32),
                                  ALU.subtract).then_inc(lo_done, 1)

            def max_item(b, q, m):
                at = MAXES * q + m
                dve.wait_ge(mx_ready, b.count(PAIRS * MAXES, at + 1 + START))
                dve.tensor_reduce(mxc[:, q % 2, m:m + 1], mx[MAX_BANK[at]][:, :], AX.X, ALU.max).then_inc(mx_done, 1)
                if m == MAXES - 1:
                    n = b.count(3 * PAIRS, 3 * q + START)
                    dve.wait_ge(mx_done, b.count(PAIRS * MAXES, at + 1 + START))
                    dve.tensor_reduce(mm[:, :], mxc[:, q % 2, :].rearrange("p (a c) -> p a c", c=QC), AX.X,
                                      ALU.max).then_inc(comb_done, 1)
                    if not (b.first and q == 0):
                        dve.wait_ge(mt_ready, b.count(PAIRS, q + START))
                    dve.wait_ge(comb_done, n + 1)
                    dve.tensor_scalar(nm[:, 0, :], mm[:, :], -1.0, None, ALU.mult).then_inc(comb_done, 1)
                    dve.wait_ge(comb_done, n + 2)
                    dve.scalar_tensor_tensor(out=nm[:, 1, :], in0=mm[:, :], scalar=-1.0, in1=nm[:, 0, :].bitcast(f32),
                                             op0=ALU.mult, op1=ALU.subtract).then_inc(comb_done, 1)

            def first_add(b, p, i):
                unit = UNITS * p + 2 + i
                dve.wait_ge(exp_done, b.count(PAIRS * SCORES, QC * (unit + 1) + START))
                dve.wait_ge(den_done, b.count(PAIRS, p + START))
                dve.tensor_tensor(Psum[:, i, :], P[:, BUFFER[unit - 2], :], P[:, BUFFER[unit], :],
                                  ALU.add).then_inc(first_added, 1)

            def reciprocal_piece(b, p, n):
                dve.wait_ge(den_copied, b.count(PAIRS, p + 1 + START))
                dve.reciprocal(rden[:, 128 * n:128 * n + 128], rden[:, 128 * n:128 * n + 128]).then_inc(rden_done, 1)

            def normalise(b, p):
                dve.wait_ge(rden_done, b.count(PAIRS * 4, 4 * p + 4 + START))
                dve.wait_ge(pv_copied, b.count(PAIRS, p + 1 + START))
                if p == 0:
                    dve.wait_ge(o_ready, b.count(KB, START))
                for c in range(QC):
                    dve.tensor_tensor(attT[64 * (p % 2):64 * (p % 2) + 64, p // 2, 512 * c:512 * c + 512],
                                      pv_s[64 * c:64 * c + 64, :], rden[64 * c:64 * c + 64, :],
                                      ALU.mult).then_inc(norm_done, 1)

            def statistics(b, n, t):
                at = b.count(2 * KB, n * KB + t + 1 + START)
                dve.bn_stats(stats[:, t, :], r[:, t, :]).then_inc(stats_done, 1)
                if t % HALF == HALF - 1:
                    dve.wait_ge(stats_done, at)
                    dve.memset(settle[:, :], 0.0)
                    for tile in range(t - HALF + 1, t + 1):
                        done = dve.bn_aggr(mv[:, tile, :], stats[:, tile, :])
                    done.then_inc(mv_done, 1)

            def residual_part(t, bank):
                if t == 0:
                    dve.wait_ge(r_loaded, final.count(16, 16))
                dve.wait_ge(part_ready, t + 1 + START)
                dve.tensor_tensor(r[:, t, :], bank[:, :], r[:, t, :], ALU.add).then_inc(part_read, 1)

            def residual_attention(b, t, bank):
                if t == 0:
                    dve.wait_ge(r_loaded, b.count(16, 16))
                dve.wait_ge(o_ready, b.count(KB, t + 1 + START))
                dve.tensor_tensor(r[:, t, :], bank[:, :], r[:, t, :], ALU.add).then_inc(o_read, 1)
                dve.wait_ge(o_read, b.count(KB, t + 1 + START))
                statistics(b, 0, t)

            def residual_experts(b, t, bank):
                dve.wait_ge(z_ready, b.count(KB, t + 1 + START))
                dve.tensor_tensor(r[:, t, :], bank[:, :], r[:, t, :], ALU.add).then_inc(z_read, 1)
                dve.wait_ge(z_read, b.count(KB, t + 1 + START))
                statistics(b, 1, t)

            def layer_norm(b, n, t):
                dve.wait_ge(rstd_done, b.count(4, 2 * n + t // HALF + 1 + START))
                dve.tensor_scalar(r[:, t, :], r[:, t, :], mv[:, t, 0:1], rstd[:, t:t + 1], ALU.subtract,
                                  ALU.mult).then_inc((y_done, out_done)[n], 1)

            def largest_logit(b, t):
                at = b.count(KB * GATE_STEPS, t * GATE_STEPS + START)
                dve.wait_ge(h_ready, b.count(KB, t + 1 + START))
                dve.tensor_reduce(lmax[:, :], den[:, 0:E], AX.X, ALU.max).then_inc(gate_step, 1)
                dve.wait_ge(gate_step, at + 1)
                dve.tensor_scalar(nlmax[:, :], lmax[:, :], -1.0, None, ALU.mult).then_inc(nlmax_done, 1)

            def gates(b, t):
                at = b.count(KB * GATE_STEPS, t * GATE_STEPS + START)
                dve.wait_ge(lexp_done, b.count(KB, t + 1 + START))
                dve.reciprocal(lrec[:, :], lsum[:, :]).then_inc(gate_step, 1)
                dve.scalar_tensor_tensor(out=eq[:, :], in0=den[:, 0:E], scalar=lmax[:, :], in1=rank[:, :],
                                         op0=ALU.is_ge, op1=ALU.mult).then_inc(gate_step, 1)
                dve.wait_ge(gate_step, at + 3)
                dve.tensor_reduce(eqm[:, :], eq[:, :], AX.X, ALU.max).then_inc(gate_step, 1)
                dve.wait_ge(gate_step, at + 4)
                dve.tensor_scalar(gate[:, :], eq[:, :], eqm[:, :], lrec[:, :], ALU.is_equal,
                                  ALU.mult).then_inc(gate_step, 1)
                dve.wait_ge(h_copied, b.count(KB, t + 1 + START))
                dve.wait_ge(gate_step, at + 5)
                dve.scalar_tensor_tensor(out=hm[:, :].rearrange("p (e r) -> p e r", e=E),
                                         in0=hm[:, :].rearrange("p (e r) -> p e r", e=E), scalar=SCALING,
                                         in1=gate[:, :].unsqueeze(2).to_broadcast([128, E, R]),
                                         op0=ALU.mult, op1=ALU.mult).then_inc(hm_done, 1)

            def slot(b, p, tail, opening, more):
                at = PLAN[tail, not more]
                last = before(b, p)
                for k in range(UNITS):
                    if more or p + 1 < PAIRS:
                        for m in max_items(at, p, k):
                            max_item(*after(b, p), m)
                    if k in ADD_AT:
                        first_add(b, p, ADD_AT.index(k))
                    if k == 0 and not (opening and p < 2):
                        normalise(*before(*last))
                    if k in REC_AT and not (opening and p == 0):
                        for n in range(2):
                            reciprocal_piece(*last, 2 * REC_AT.index(k) + n)
                    if tail and (p, k) in GATES_AT:
                        gates(b - 1, GATES_AT[p, k])
                    kind, n = at.get((p, k), (None, None))
                    if kind == "qk" and (more or p < 6):
                        lo_part(b + (p == 6), QK_SLOTS[p], n, w)
                    elif kind == "o_part":
                        residual_part(n, w)
                    elif kind == "o":
                        residual_attention(b - 1, n, w)
                    elif kind == "h":
                        largest_logit(b - 1, n)
                    elif kind == "z":
                        residual_experts(b - 1, n, w)
                    if tail and (p, k) in LN_APPLY:
                        layer_norm(b - 1, *LN_APPLY[p, k])

            start(dve, part_read, first_added, lo_done, mx_done, comb_done, rden_done, norm_done, o_read, stats_done, mv_done, y_done,
                  nlmax_done, gate_step, hm_done, z_read, out_done)
            dve.memset(stacks[3 * HD:KS, :, 0, :, :].bitcast(f32), 1.0).then_inc(const_ready, 1)
            dve.memset(ones[:, :], 1.0).then_inc(const_ready, 1)
            dve.memset(ones_row[:, :], 1.0).then_inc(const_ready, 1)
            for e in range(E):
                dve.memset(rank[:, e:e + 1], float(E - e)).then_inc(const_ready, 1)
            dve.wait_ge(const_ready, CONSTS)
            for n in range(4):
                lo_part(first, 0, n, (w, pv)[n % 2])
            for m in range(MAXES):
                max_item(first, 0, m)
            for p in range(SPLIT):
                slot(first, p, False, True, True)
            with dve.Fori(0, B - 1) as i:
                b = Batch(i)
                for p in range(SPLIT, PAIRS):
                    slot(Batch(fresh(dve, i)), p, True, False, True)
                for p in range(SPLIT):
                    slot(Batch(fresh(dve, i), 1), p, True, False, True)
            for p in range(SPLIT, PAIRS):
                slot(final, p, True, False, False)
            normalise(final, PAIRS - 2)
            for n in range(4):
                reciprocal_piece(final, PAIRS - 1, n)
            normalise(final, PAIRS - 1)
            for kind, t in last_tail():
                if kind == "o":
                    residual_attention(final, t, o_bank(t))
                    if t % HALF == HALF - 1:
                        for tile in range(t - HALF + 1, t + 1):
                            layer_norm(final, 0, tile)
                if kind == "h":
                    largest_logit(final, t)
                    gates(final, t)
                elif kind == "z":
                    residual_experts(final, t, LAST_BANK[kind])
                    if t % HALF == HALF - 1:
                        for tile in range(t - HALF + 1, t + 1):
                            layer_norm(final, 1, tile)


def kernel(L0_attn_x, L0_attn_wq, L0_attn_wk, L0_attn_wv, L0_attn_wo, L0_ffn_A, L0_ffn_B, L0_ffn_Wr, L0_ffn_br):
    import numpy as np
    import concourse.bacc as bacc
    from concourse.bass_utils import run_bass_kernel_spmd

    x = np.asarray(L0_attn_x)
    d = x.shape[-1]
    e, r = L0_ffn_A.shape[:2]
    arrays = {
        "xT": np.ascontiguousarray(x.reshape(-1, d).T),
        "x": np.ascontiguousarray(x),
        "wqT": np.ascontiguousarray(np.asarray(L0_attn_wq).T),
        "wkT": np.ascontiguousarray(np.asarray(L0_attn_wk).T),
        "wvT": np.ascontiguousarray(np.asarray(L0_attn_wv).T),
        "woT": np.ascontiguousarray(np.asarray(L0_attn_wo).T),
        "aT": np.ascontiguousarray(np.asarray(L0_ffn_A).reshape(e * r, d).T),
        "bT": np.ascontiguousarray(np.asarray(L0_ffn_B).transpose(0, 2, 1).reshape(e * r, d)),
        "wrT": np.ascontiguousarray(np.asarray(L0_ffn_Wr).T),
        "br": np.ascontiguousarray(np.asarray(L0_ffn_br).reshape(1, e)),
    }
    nc = bacc.Bacc("TRN2", target_bir_lowering=False, num_devices=1)
    args = [nc.dram_tensor(n, a.shape, mybir.dt.from_np(a.dtype), kind="ExternalInput").ap() for n, a in arrays.items()]
    out = nc.dram_tensor("out", x.shape, mybir.dt.float32, kind="ExternalOutput").ap()
    build_attention_lora_moe_block(nc, *args, out)
    result = run_bass_kernel_spmd(nc, [arrays], core_ids=[0])
    return result.results[0]["out"]
```
